# Optimizing a Trainium2 kernel written in Bass

```python
import numpy as np
import jax
import jax.numpy as jnp

def _softmax(x, axis=-1):
    return jax.nn.softmax(x, axis=axis)

def _gelu(x):
    return jax.nn.gelu(x, approximate=True)

def _silu(x):
    return jax.nn.silu(x)

def _sigmoid(x):
    return jax.nn.sigmoid(x)

def _layernorm(x, axis=-1, eps=1e-05):
    m = jnp.mean(x, axis=axis, keepdims=True)
    v = jnp.var(x, axis=axis, keepdims=True)
    return (x - m) / jnp.sqrt(v + eps)

def _scatter_add(tgt, idx, src, axis=0):
    return tgt.at[idx].add(src)

def _segment_sum(src, seg, n):
    return jax.ops.segment_sum(src, seg, n)
kernel_name = 'mk_hybrid_d1_jaxref_r8_ac1341'

def setup_inputs(seed: int=0):
    np.random.seed(seed)
    _w = jnp.asarray

    def _L0_attn_a_setup():
        import jax, jax.numpy as jnp
        import numpy as np
        DIM = 128
        INNER = DIM // 2
        DSTATE = 8
        KSZ = 3
        DTRANK = max(INNER // 8, 4)
        B, L = (4, 512)

        def _dwconv_silu(u, kern):
            c = u.shape[-1]
            v = jnp.transpose(u, (0, 2, 1))
            v = jax.lax.conv_general_dilated(v, kern, (1,), [(KSZ // 2, KSZ // 2)], dimension_numbers=('NCH', 'OIH', 'NCH'), feature_group_count=c)
            return jax.nn.silu(jnp.transpose(v, (0, 2, 1)))

        def _forward(x, W_in, Kx, Kz, W_xproj, W_dt, b_dt, A_log, D, W_out):
            h = jnp.einsum('bld,ed->ble', x, W_in)
            xb, zb = jnp.split(h, 2, axis=-1)
            xb = _dwconv_silu(xb, Kx)
            zb = _dwconv_silu(zb, Kz)
            proj = jnp.einsum('blc,oc->blo', xb, W_xproj)
            dt_raw = proj[..., :DTRANK]
            b_raw = proj[..., DTRANK:DTRANK + DSTATE]
            c_raw = proj[..., DTRANK + DSTATE:]
            delta = jnp.clip(jax.nn.softplus(jnp.einsum('blr,cr->blc', dt_raw, W_dt) + b_dt), 0.0001, 1.0)
            b_term = jnp.tanh(b_raw)
            c_term = jnp.tanh(c_raw)
            a = jax.nn.softplus(A_log) + 0.0001
            decay = jnp.clip(jnp.exp(-delta[..., None] * a), 0.0001, 1.0)
            drive = (1.0 - decay) * (b_term[:, :, None, :] * xb[..., None])

            def step(state, inp):
                dec_t, drv_t, c_t, x_t = inp
                state = dec_t * state + drv_t
                y = jnp.sum(state * c_t[:, None, :], axis=-1) + D * x_t
                return (state, y)
            tm = lambda t: jnp.moveaxis(t, 1, 0)
            state0 = jnp.zeros((x.shape[0], INNER, DSTATE), dtype=jnp.float32)
            _, ys = jax.lax.scan(step, state0, (tm(decay), tm(drive), tm(c_term), tm(xb)))
            y = jnp.moveaxis(ys, 0, 1)
            return jnp.einsum('bld,ed->ble', jnp.concatenate([y, zb], axis=-1), W_out)
        key = jax.random.key(seed)
        ks = jax.random.split(key, 8)
        s = 0.02
        x = jax.random.normal(ks[0], (B, L, DIM), dtype=jnp.float32)
        W_in = jax.random.normal(ks[1], (DIM, DIM), dtype=jnp.float32) * s
        Kx = jax.random.normal(ks[2], (INNER, 1, KSZ), dtype=jnp.float32) * 0.1
        Kz = jax.random.normal(ks[3], (INNER, 1, KSZ), dtype=jnp.float32) * 0.1
        W_xproj = jax.random.normal(ks[4], (DTRANK + 2 * DSTATE, INNER), dtype=jnp.float32) * s
        W_dt = jax.random.normal(ks[5], (INNER, DTRANK), dtype=jnp.float32) * s
        dt_init = jnp.exp(jnp.linspace(jnp.log(0.02), jnp.log(0.2), INNER))
        b_dt = jnp.log(jnp.expm1(dt_init)).astype(jnp.float32)
        A_log = jnp.log(jnp.tile(jnp.arange(1, DSTATE + 1, dtype=jnp.float32), (INNER, 1)))
        D = jnp.ones((INNER,), dtype=jnp.float32)
        W_out = jax.random.normal(ks[6], (DIM, DIM), dtype=jnp.float32) * s
        return {'x': x, 'W_in': W_in, 'Kx': Kx, 'Kz': Kz, 'W_xproj': W_xproj, 'W_dt': W_dt, 'b_dt': b_dt, 'A_log': A_log, 'D': D, 'W_out': W_out}
    _L0_attn_a_in = _L0_attn_a_setup()

    def _L0_attn_b_setup():
        import jax, jax.numpy as jnp
        import numpy as np
        EMBED_DIM = 128
        NUM_HEADS = 16
        HEAD_DIM = EMBED_DIM // NUM_HEADS
        CHUNK_SIZE = 10
        LEFT_CONTEXT = 25
        RIGHT_CONTEXT = 0
        NEG_INF = -1e+30

        def chunk_attention_mask(seq_len: int) -> jnp.ndarray:
            i = jnp.arange(seq_len)[:, None]
            j = jnp.arange(seq_len)[None, :]
            chunk_start = i // CHUNK_SIZE * CHUNK_SIZE
            chunk_end = jnp.minimum(chunk_start + CHUNK_SIZE, seq_len)
            in_chunk = (j >= chunk_start) & (j < chunk_end)
            in_left = (j >= i - LEFT_CONTEXT) & (j < chunk_start)
            in_right = (j >= chunk_end) & (j < jnp.minimum(seq_len, i + RIGHT_CONTEXT + 1))
            allowed = in_chunk | in_left | in_right
            return jnp.where(allowed, 0.0, NEG_INF).astype(jnp.float32)
        key = jax.random.key(seed)
        ks = jax.random.split(key, 9)
        B, S, E = (2, 256, EMBED_DIM)
        s = 1.0 / np.sqrt(E)
        return {'hidden_states': jax.random.normal(ks[0], (B, S, E), jnp.float32), 'Wq': jax.random.normal(ks[1], (E, E), jnp.float32) * s, 'bq': jax.random.normal(ks[2], (E,), jnp.float32) * 0.02, 'Wk': jax.random.normal(ks[3], (E, E), jnp.float32) * s, 'bk': jax.random.normal(ks[4], (E,), jnp.float32) * 0.02, 'Wv': jax.random.normal(ks[5], (E, E), jnp.float32) * s, 'bv': jax.random.normal(ks[6], (E,), jnp.float32) * 0.02, 'Wo': jax.random.normal(ks[7], (E, E), jnp.float32) * s, 'bo': jax.random.normal(ks[8], (E,), jnp.float32) * 0.02}
    _L0_attn_b_in = _L0_attn_b_setup()

    def _L0_ffn_setup():
        import jax, jax.numpy as jnp
        import numpy as np
        B, S, H = (2, 128, 128)
        E, F = (8, 512)
        GATE_TEMP = 0.1
        key = jax.random.key(seed)
        ks = jax.random.split(key, 6)
        s_h = 1.0 / np.sqrt(H)
        s_f = 1.0 / np.sqrt(F)
        return {'hidden_states': jax.random.normal(ks[0], (B, S, H), dtype=jnp.float32), 'w_router': jax.random.normal(ks[1], (H, E), dtype=jnp.float32) * s_h, 'w_gating': jax.random.normal(ks[2], (H, E), dtype=jnp.float32) * s_h, 'w_gate': jax.random.normal(ks[3], (E, H, F), dtype=jnp.float32) * s_h, 'w_up': jax.random.normal(ks[4], (E, H, F), dtype=jnp.float32) * s_h, 'w_down': jax.random.normal(ks[5], (E, F, H), dtype=jnp.float32) * s_f}
    _L0_ffn_in = _L0_ffn_setup()
    _d = {'L0_attn_a_x': _L0_attn_a_in['x'], 'L0_attn_a_W_in': _L0_attn_a_in['W_in'], 'L0_attn_a_Kx': _L0_attn_a_in['Kx'], 'L0_attn_a_Kz': _L0_attn_a_in['Kz'], 'L0_attn_a_W_xproj': _L0_attn_a_in['W_xproj'], 'L0_attn_a_W_dt': _L0_attn_a_in['W_dt'], 'L0_attn_a_b_dt': _L0_attn_a_in['b_dt'], 'L0_attn_a_A_log': _L0_attn_a_in['A_log'], 'L0_attn_a_D': _L0_attn_a_in['D'], 'L0_attn_a_W_out': _L0_attn_a_in['W_out'], 'L0_attn_b_Wq': _L0_attn_b_in['Wq'], 'L0_attn_b_bq': _L0_attn_b_in['bq'], 'L0_attn_b_Wk': _L0_attn_b_in['Wk'], 'L0_attn_b_bk': _L0_attn_b_in['bk'], 'L0_attn_b_Wv': _L0_attn_b_in['Wv'], 'L0_attn_b_bv': _L0_attn_b_in['bv'], 'L0_attn_b_Wo': _L0_attn_b_in['Wo'], 'L0_attn_b_bo': _L0_attn_b_in['bo'], 'L0_ffn_w_router': _L0_ffn_in['w_router'], 'L0_ffn_w_gating': _L0_ffn_in['w_gating'], 'L0_ffn_w_gate': _L0_ffn_in['w_gate'], 'L0_ffn_w_up': _L0_ffn_in['w_up'], 'L0_ffn_w_down': _L0_ffn_in['w_down']}
    _x0 = _d['L0_attn_a_x']
    _d['L0_attn_a_x'] = jax.random.normal(jax.random.fold_in(jax.random.key(seed), 1), (8, 512, 128), dtype=_x0.dtype)
    del _x0
    return _d

def reference(L0_attn_a_x, L0_attn_a_W_in, L0_attn_a_Kx, L0_attn_a_Kz, L0_attn_a_W_xproj, L0_attn_a_W_dt, L0_attn_a_b_dt, L0_attn_a_A_log, L0_attn_a_D, L0_attn_a_W_out, L0_attn_b_Wq, L0_attn_b_bq, L0_attn_b_Wk, L0_attn_b_bk, L0_attn_b_Wv, L0_attn_b_bv, L0_attn_b_Wo, L0_attn_b_bo, L0_ffn_w_router, L0_ffn_w_gating, L0_ffn_w_gate, L0_ffn_w_up, L0_ffn_w_down):

    def _L0_attn_a_ref(x, W_in, Kx, Kz, W_xproj, W_dt, b_dt, A_log, D, W_out):
        import jax, jax.numpy as jnp
        import numpy as np
        DIM = 128
        INNER = DIM // 2
        DSTATE = 8
        KSZ = 3
        DTRANK = max(INNER // 8, 4)
        B, L = (4, 512)

        def _dwconv_silu(u, kern):
            c = u.shape[-1]
            v = jnp.transpose(u, (0, 2, 1))
            v = jax.lax.conv_general_dilated(v, kern, (1,), [(KSZ // 2, KSZ // 2)], dimension_numbers=('NCH', 'OIH', 'NCH'), feature_group_count=c)
            return jax.nn.silu(jnp.transpose(v, (0, 2, 1)))

        def _forward(x, W_in, Kx, Kz, W_xproj, W_dt, b_dt, A_log, D, W_out):
            h = jnp.einsum('bld,ed->ble', x, W_in)
            xb, zb = jnp.split(h, 2, axis=-1)
            xb = _dwconv_silu(xb, Kx)
            zb = _dwconv_silu(zb, Kz)
            proj = jnp.einsum('blc,oc->blo', xb, W_xproj)
            dt_raw = proj[..., :DTRANK]
            b_raw = proj[..., DTRANK:DTRANK + DSTATE]
            c_raw = proj[..., DTRANK + DSTATE:]
            delta = jnp.clip(jax.nn.softplus(jnp.einsum('blr,cr->blc', dt_raw, W_dt) + b_dt), 0.0001, 1.0)
            b_term = jnp.tanh(b_raw)
            c_term = jnp.tanh(c_raw)
            a = jax.nn.softplus(A_log) + 0.0001
            decay = jnp.clip(jnp.exp(-delta[..., None] * a), 0.0001, 1.0)
            drive = (1.0 - decay) * (b_term[:, :, None, :] * xb[..., None])

            def step(state, inp):
                dec_t, drv_t, c_t, x_t = inp
                state = dec_t * state + drv_t
                y = jnp.sum(state * c_t[:, None, :], axis=-1) + D * x_t
                return (state, y)
            tm = lambda t: jnp.moveaxis(t, 1, 0)
            state0 = jnp.zeros((x.shape[0], INNER, DSTATE), dtype=jnp.float32)
            _, ys = jax.lax.scan(step, state0, (tm(decay), tm(drive), tm(c_term), tm(xb)))
            y = jnp.moveaxis(ys, 0, 1)
            return jnp.einsum('bld,ed->ble', jnp.concatenate([y, zb], axis=-1), W_out)
        return _forward(x, W_in, Kx, Kz, W_xproj, W_dt, b_dt, A_log, D, W_out)

    def _L0_attn_b_ref(hidden_states, Wq, bq, Wk, bk, Wv, bv, Wo, bo):
        import jax, jax.numpy as jnp
        import numpy as np
        EMBED_DIM = 128
        NUM_HEADS = 16
        HEAD_DIM = EMBED_DIM // NUM_HEADS
        CHUNK_SIZE = 10
        LEFT_CONTEXT = 25
        RIGHT_CONTEXT = 0
        NEG_INF = -1e+30

        def chunk_attention_mask(seq_len: int) -> jnp.ndarray:
            i = jnp.arange(seq_len)[:, None]
            j = jnp.arange(seq_len)[None, :]
            chunk_start = i // CHUNK_SIZE * CHUNK_SIZE
            chunk_end = jnp.minimum(chunk_start + CHUNK_SIZE, seq_len)
            in_chunk = (j >= chunk_start) & (j < chunk_end)
            in_left = (j >= i - LEFT_CONTEXT) & (j < chunk_start)
            in_right = (j >= chunk_end) & (j < jnp.minimum(seq_len, i + RIGHT_CONTEXT + 1))
            allowed = in_chunk | in_left | in_right
            return jnp.where(allowed, 0.0, NEG_INF).astype(jnp.float32)
        B, S, E = hidden_states.shape
        H, D = (NUM_HEADS, HEAD_DIM)
        scaling = D ** (-0.5)

        def proj(x, W, b):
            y = jnp.einsum('bse,fe->bsf', x, W) + b
            return y.reshape(B, S, H, D).transpose(0, 2, 1, 3)
        q = proj(hidden_states, Wq, bq) * scaling
        k = proj(hidden_states, Wk, bk)
        v = proj(hidden_states, Wv, bv)
        scores = jnp.einsum('bhsd,bhtd->bhst', q, k)
        scores = scores + chunk_attention_mask(S)[None, None]
        probs = jax.nn.softmax(scores, axis=-1)
        out = jnp.einsum('bhst,bhtd->bhsd', probs, v)
        out = out.transpose(0, 2, 1, 3).reshape(B, S, E)
        out = jnp.einsum('bse,fe->bsf', out, Wo) + bo
        return out

    def _L0_ffn_ref(hidden_states, w_router, w_gating, w_gate, w_up, w_down):
        import jax, jax.numpy as jnp
        import numpy as np
        B, S, H = (2, 128, 128)
        E, F = (8, 512)
        GATE_TEMP = 0.1
        x = hidden_states
        router_probs = jax.nn.softmax(jnp.einsum('bsh,he->bse', x, w_router), axis=-1)
        gate_weights = jax.nn.softmax(jnp.einsum('bsh,he->bse', x, w_gating) / GATE_TEMP, axis=-1)
        g = jnp.einsum('bsh,ehf->ebsf', x, w_gate)
        u = jnp.einsum('bsh,ehf->ebsf', x, w_up)
        h = jax.nn.silu(g) * u
        expert_out = jnp.einsum('ebsf,efh->ebsh', h, w_down)
        cw = router_probs * gate_weights
        cw = cw / (jnp.sum(cw, axis=-1, keepdims=True) + 1e-09)
        out = jnp.einsum('ebsh,bse->bsh', expert_out, cw)
        return out
    x = L0_attn_a_x
    x = x + _L0_attn_a_ref(_layernorm(x, axis=-1), L0_attn_a_W_in, L0_attn_a_Kx, L0_attn_a_Kz, L0_attn_a_W_xproj, L0_attn_a_W_dt, L0_attn_a_b_dt, L0_attn_a_A_log, L0_attn_a_D, L0_attn_a_W_out)
    x = x + _L0_ffn_ref(_layernorm(x, axis=-1), L0_ffn_w_router, L0_ffn_w_gating, L0_ffn_w_gate, L0_ffn_w_up, L0_ffn_w_down)
    x = x + _L0_attn_b_ref(_layernorm(x, axis=-1), L0_attn_b_Wq, L0_attn_b_bq, L0_attn_b_Wk, L0_attn_b_bk, L0_attn_b_Wv, L0_attn_b_bv, L0_attn_b_Wo, L0_attn_b_bo)
    x = x + _L0_ffn_ref(_layernorm(x, axis=-1), L0_ffn_w_router, L0_ffn_w_gating, L0_ffn_w_gate, L0_ffn_w_up, L0_ffn_w_down)
    return x

_drawn_inputs = setup_inputs


def setup_inputs(seed=0):
    import zlib

    import numpy as np

    out = dict(_drawn_inputs(seed))
    spreads = {'L0_attn_a_D': (1.0, 0.6)}
    factors = {'L0_attn_a_W_in': 5.455,
     'L0_attn_a_Kx': 7.664,
     'L0_attn_a_Kz': 8.0,
     'L0_attn_a_W_xproj': 8.0,
     'L0_attn_a_W_dt': 54.821,
     'L0_attn_a_b_dt': 54.564,
     'L0_attn_a_A_log': 8.0,
     'L0_attn_a_W_out': 5.311,
     'L0_attn_b_bq': 22.386,
     'L0_attn_b_bk': 64.0,
     'L0_attn_b_bv': 4.128,
     'L0_attn_b_bo': 4.282}
    for name, (base, spread) in spreads.items():
        noise = np.random.default_rng([zlib.crc32(name.encode()), seed]).standard_normal(out[name].shape)
        drawn = base * np.exp(spread * noise) if base else spread * noise
        out[name] = jnp.asarray(drawn.astype(out[name].dtype))
    for name, factor in factors.items():
        out[name] = (out[name] * factor).astype(out[name].dtype)
    return out
```

```python
import contextlib

import numpy as np

import concourse.bass as bass
from concourse import mybir
from concourse.alu_op_type import AluOpType as ALU

F32 = mybir.dt.float32
F32R = mybir.dt.float32r
ACT = mybir.ActivationFunctionType
AX = mybir.AxisListType.X

B, L, D = 8, 512, 128
P = 128
TT = L // P
INNER, DSTATE, DTRANK = 64, 8, 8
KT = INNER * DSTATE // P
HEADS, HD = 16, 8
CHUNK, LEFT = 10, 25
QT = 100
NQT = -(-L // QT)
KW = QT + LEFT + 1
E, F = 8, 512
NCH = E * F // P
CPE = F // P
LAG = 3
EPS = 1e-5
NEG = -1e30

_COLS = {}


def _layout():
    at = 0
    for name, n in (("w_bc", 16), ("w_dtx", 128), ("w_dt", 128), ("w_q", 128), ("w_k", 128), ("w_v", 128),
                    ("w_in", 128), ("k_conv", 3),
                    ("b_dt", 1), ("a_log", KT), ("d_skip", 1), ("w_out_y", 128), ("w_out_z", 128),
                    ("w_route", 2 * E), ("b_q", 4), ("b_k", 4),
                    ("b_v", 128), ("w_o", 128), ("b_o", 128), ("ident", 128),
                    ("mask", KW), ("sel", E), ("lo_ssm", 1), ("lo_q", 1),
                    ("lo_k", 1)):
        _COLS[name] = (at, n)
        at += n
    return at


NPACK = _layout()
NRAW = _COLS["w_in"][0]


def build(nc, x_d, pack_d, wg_d, wu_d, wd_d, out_d):
    ctx = contextlib.ExitStack()
    with ctx:
        def sb(name, shape, dt=F32):
            return ctx.enter_context(nc.sbuf_tensor(name, shape, dt))

        def sem(name):
            s = ctx.enter_context(nc.semaphore(name))
            sems.append(s)
            return s

        sems = []
        pack = sb("pack", [P, NPACK - NRAW])

        def pk(name):
            at, n = _COLS[name]
            return pack[:, at - NRAW:at - NRAW + n] if at >= NRAW else raw[:, at:at + n]

        sel = sb("sel", [32 + 2 * E, E], F32R)
        wg = [sb(f"w_gate_{v}", [P, NCH, P], F32R) for v in ("hi", "lo")]
        wu = [sb(f"w_up_{v}", [P, NCH, P], F32R) for v in ("hi", "lo")]
        wd = [sb(f"w_down_{v}", [P, NCH, P], F32R) for v in ("hi", "lo")]
        wq = [sb(f"w_q_{v}", [P, 4, 4, 4, HD], F32R) for v in ("hi", "lo")]
        wk = [sb(f"w_k_{v}", [P, 4, 4, 4, HD], F32R) for v in ("hi", "lo")]
        wv = [sb(f"w_v_{v}", [P, P], F32R) for v in ("hi", "lo")]
        wbc = [sb(f"w_bc_{v}", [P, 2 * DSTATE, INNER], F32R) for v in ("hi", "lo")]
        wdt = [sb(f"w_dt_{v}", [P, P], F32R) for v in ("hi", "lo")]
        neg_a = sb("neg_a", [P, KT])
        bq_lo = sb("bq_lo", [P, 8])
        half = sb("half", [P, TT])

        x1 = sb("x1", [P, TT, D])
        x2 = sb("x2", [P, TT, D])
        x3 = sb("x3", [P, TT, D])
        ffn_out = sb("ffn_out", [P, L])

        fx = [sb(f"ffn_x{s}", [P, L]) for s in range(2)]
        fxh = [sb(f"ffn_x_hi{s}", [P, L], F32R) for s in range(2)]
        fxl = [sb(f"ffn_x_lo{s}", [P, L], F32R) for s in range(2)]
        mixT = sb("mix_t", [32 + 2 * E, L], F32R)
        cwT = [mixT[32 * s:32 * s + 2 * E, :] for s in range(2)]

        h_b = sb("h", [P, 3, L])
        hh_b = sb("h_hi", [P, 3, L], F32R)
        hl_b = sb("h_lo", [P, 3, L], F32R)
        xe = sb("xe", [P, L])
        xeh = sb("xe_hi", [P, 2, L], F32R)
        xel = sb("xe_lo", [P, 2, L], F32R)

        bn6 = sb("bn6", [P, TT, 6])
        mv = sb("mv", [P, TT, 2])
        rstd = sb("rstd", [P, TT])
        lg = sb("route", [P, TT, 2, E])
        lmax = sb("route_max", [P, TT, 2])
        cw = sb("mix", [P, TT, E])
        cws = sb("mix_sums", [P, TT, 2])
        cwh = sb("mix_hi", [P, TT, E], F32R)
        cwhl = sb("mix_hi_lo", [P, TT, 2 * E])
        arena = sb("arena", [P, 9, L])
        xb2, zb, delta, tot, cv, sxT = (arena[:, i, :] for i in range(6))
        btile, ctile = arena[:, 6, :], arena[:, 7:9, :]
        dec = arena[:, 4:6, :]
        xn = arena[:, 0, :].rearrange("p (t d) -> p t d", t=TT)
        flat = arena[:, :, :].rearrange("p a b -> p (a b)")
        raw = flat[:, 7 * L:7 * L + NRAW]
        NU = 8 * KW
        s_u = [flat[:, i * NU:(i + 1) * NU].rearrange("p (r g k) -> p r g k", r=2, g=4) for i in range(2)]
        pt_u = flat[:, 2 * NU:2 * NU + 8 * QT].rearrange("p (r g q) -> p r g q", r=2, g=4)
        o1 = 2 * NU + 8 * QT
        v_t = flat[:, o1:o1 + NQT * HEADS * 9].rearrange("p (t h e) -> p t h e", t=NQT, e=9)
        o1 += NQT * HEADS * 9
        att = flat[:, o1:o1 + NQT * D].rearrange("p (t e) -> p t e", t=NQT)
        o1 += NQT * D
        attT = flat[:, 0:L]
        smax = flat[:, o1:o1 + 8].rearrange("p (r g) -> p r g", r=2)
        rinv = flat[:, o1 + 8:o1 + 16].rearrange("p (r g) -> p r g", r=2)
        assert o1 + 16 <= 9 * L
        XW = L + 2
        axh = sb("attn_x_hi", [P, XW], F32R)
        axl = sb("attn_x_lo", [P, XW], F32R)
        q3 = sb("q3", [P, 4, L], F32R)
        k3 = sb("k3", [P, 4, XW], F32R)
        xs = axl[:, 0:L]
        xsm = axh[:, 0:L]

        pg = [ctx.enter_context(nc.psum_tensor(f"pg{i}", [P, L], F32)) for i in range(2)]
        pu = [ctx.enter_context(nc.psum_tensor(f"pu{i}", [P, L], F32)) for i in range(2)]
        pd = ctx.enter_context(nc.psum_tensor("pd", [P, L], F32))
        pb = ctx.enter_context(nc.psum_tensor("pb", [P, L], F32))
        side_ps = [ctx.enter_context(nc.psum_tensor(f"ps{i}", [P, L], F32)) for i in range(2)]

        loaded, packed, stored = sem("loaded"), sem("packed"), sem("stored")
        w_loaded = [sem(f"w_loaded{i}") for i in range(3)]
        w_hi, w_lo, w_small, w_prep = sem("w_hi"), sem("w_lo"), sem("w_small"), sem("w_prep")
        g_full, u_full, silu_done, h_done = sem("g_full"), sem("u_full"), sem("silu_done"), sem("h_done")
        hh_done, hl_done, down_done, ffn_ready = sem("hh_done"), sem("hl_done"), sem("down_done"), sem("ffn_ready")
        mix_full, xe_done, xeh_done, xel_done = sem("mix_full"), sem("xe_done"), sem("xeh_done"), sem("xel_done")
        bank_full = [sem("bank_full0"), sem("bank_full1")]
        bank_free = [sem("bank_free0"), sem("bank_free1")]
        finished = sem("finished")
        ln_stats, ln_rstd, ln_out = sem("ln_stats"), sem("ln_rstd"), sem("ln_out")
        x_hi, x_lo, x_f32 = sem("x_hi"), sem("x_lo"), sem("x_f32")
        logits, route_exp, mix_ready, mixT_ready = sem("logits"), sem("route_exp"), sem("mix_ready"), sem("mixT_ready")
        conv_done, silu_x, xs_m, xs_done = sem("conv_done"), sem("silu_x"), sem("xs_m"), sem("xs_done")
        dt_in, dt_soft, delta_done = sem("dt_in"), sem("dt_soft"), sem("delta_done")
        b_tanh, c_tanh, bx_done, dec_exp = sem("b_tanh"), sem("c_tanh"), sem("bx_done"), sem("dec_exp")
        scan_done, y_part, y_done, x1_done = sem("scan_done"), sem("y_part"), sem("y_done"), sem("x1_done")
        q_lo_m, q_done, v_done = sem("q_lo_m"), sem("q_done"), sem("v_done")
        s_masked, s_max, s_sub, s_exp = sem("s_masked"), sem("s_max"), sem("s_sub"), sem("s_exp")
        pt_done, att_done, attT_done, x3_pre = sem("pt_done"), sem("att_done"), sem("attT_done"), sem("x3_pre")
        act_step, dve_step, pool_step = sem("act_step"), sem("dve_step"), sem("pool_step")

        class Chain:

            def __init__(self, eng, s):
                self.eng, self.s, self.n = eng, s, 0

            def __call__(self, ins):
                self.n += 1
                ins.then_inc(self.s, 1)
                self.eng.wait_ge(self.s, self.n)

        class Banks:

            def __init__(self, names):
                self.n = {name: i for i, name in enumerate(names)}

            def ps(self, name):
                return side_ps[self.n[name] % 2]

            def take(self, pe, name):
                u = self.n[name]
                if u >= 2:
                    pe.wait_ge(bank_free[u % 2], u // 2)

            def fill(self, ins, name):
                ins.then_inc(bank_full[self.n[name] % 2], 1)

            def wait(self, eng, name):
                u = self.n[name]
                eng.wait_ge(bank_full[u % 2], u // 2 + 1)

            def free(self, ins, name):
                ins.then_inc(bank_free[self.n[name] % 2], 1)

            def wait_free(self, eng, name):
                u = self.n[name]
                eng.wait_ge(bank_free[u % 2], u // 2 + 1)

        def split3(out, w, x_parts, first=True, last=True):
            nc.tensor.matmul(out, w[0], x_parts[0], start=first, stop=False)
            nc.tensor.matmul(out, w[0], x_parts[1], start=False, stop=False)
            return nc.tensor.matmul(out, w[1], x_parts[0], start=False, stop=last)

        ident = pk("ident")

        def norm_dve(dve, link, x, n):
            for t in range(TT):
                nc.vector.bn_stats(bn6[:, t, :], x[:, t, :]).then_inc(dve_step, 1)
                link.n += 1
            dve.wait_ge(dve_step, link.n)
            for t in range(TT):
                last = nc.vector.bn_aggr(mv[:, t, :], bn6[:, t, :])
                if t < TT - 1:
                    last.then_inc(dve_step, 1)
                    link.n += 1
            last.then_inc(ln_stats, 1)
            yield 1
            dve.wait_ge(ln_rstd, n + 1)
            for t in range(TT):
                nc.vector.tensor_scalar(xn[:, t, :], x[:, t, :], mv[:, t, 0:1], rstd[:, t:t + 1],
                                        ALU.subtract, ALU.mult).then_inc(ln_out, 1)

        def norm_pool(pool, link, n):
            pool.wait_ge(ln_stats, n + 1)
            link(nc.gpsimd.tensor_scalar(rstd[:, :], mv[:, :, 1], EPS, None, ALU.add))
            nc.gpsimd.tensor_tensor(rstd[:, :], rstd[:, :], half[:, :], ALU.pow).then_inc(ln_rstd, 1)

        def norm_pe(pe, banks, name, n):
            banks.take(pe, name)
            pe.wait_ge(ln_out, TT * (n + 1))
            ps = banks.ps(name)
            for t in range(TT):
                last = nc.tensor.transpose(ps[:, t * P:(t + 1) * P], xn[:, t, :], ident)
            banks.fill(last, name)

        def finish_pe(pe, banks):
            banks.take(pe, "fin")
            for t in range(TT):
                last = nc.tensor.transpose(banks.ps("fin")[:, t * P:(t + 1) * P], ffn_out[:, t * P:(t + 1) * P], ident)
            banks.fill(last, "fin")

        def finish_dve(dve, link, banks, src, dst):
            banks.wait(dve, "fin")
            ps = banks.ps("fin")
            banks.free(nc.vector.tensor_tensor(dst[:, :, :].rearrange("p t d -> p (t d)"), ps[:, :],
                                               src[:, :, :].rearrange("p t d -> p (t d)"), ALU.add), "fin")
            banks.wait_free(dve, "fin")

        def head_pe(pe, banks, slot, n):
            norm_pe(pe, banks, "ln2", n)
            yield 2
            banks.take(pe, "route")
            pe.wait_ge(x_f32, 1)
            ps = banks.ps("route")
            for t in range(TT):
                last = nc.tensor.matmul(ps[:, t * 2 * E:(t + 1) * 2 * E], fx[slot][:, t * P:(t + 1) * P],
                                        pk("w_route"), start=True, stop=True)
            banks.fill(last, "route")
            yield 4
            banks.take(pe, "mixT")
            pe.wait_ge(mix_ready, 1)
            ps = banks.ps("mixT")
            for t in range(TT):
                last = nc.tensor.transpose(ps[0:2 * E, t * P:(t + 1) * P], cwhl[:, t, :], ident)
            banks.fill(last, "mixT")

        def head_act(act, link, banks, slot):
            banks.wait(act, "ln2")
            nc.scalar.copy(fx[slot][:, :], banks.ps("ln2")[:, :]).then_inc(x_f32, 1)
            nc.scalar.copy(fxh[slot][:, :], banks.ps("ln2")[:, :]).then_inc(x_hi, 1)
            yield 2
            banks.wait_free(act, "route")
            nc.scalar.activation(lg[:, :, 0, :], lg[:, :, 0, :], ACT.Exp).then_inc(route_exp, 1)
            nc.scalar.activation(lg[:, :, 1, :], lg[:, :, 1, :], ACT.Exp, scale=10.0).then_inc(route_exp, 1)
            yield 4
            banks.wait(act, "mixT")
            banks.free(nc.scalar.copy(cwT[slot], banks.ps("mixT")[0:2 * E, :]), "mixT")

        def head_dve(dve, link, banks, slot, nxh):
            dve.wait_ge(x_hi, nxh)
            banks.free(nc.vector.tensor_tensor(fxl[slot][:, :], banks.ps("ln2")[:, :],
                                               fxh[slot][:, :].bitcast(F32), ALU.subtract), "ln2")
            yield 2
            banks.wait(dve, "route")
            lps = banks.ps("route")[:, 0:TT * 2 * E].rearrange("p (t k e) -> p t k e", t=TT, k=2)
            link(nc.vector.reduce_max(lmax[:, :, :], lps, AX))
            banks.free(nc.vector.tensor_tensor(lg[:, :, :, :], lps,
                                               lmax[:, :, :].unsqueeze(3).broadcast_to([P, TT, 2, E]), ALU.subtract), "route")
            yield 2
            dve.wait_ge(route_exp, 2)
            link(nc.vector.reduce_sum(cws[:, :, :], lg[:, :, :, :], AX))
            link(nc.vector.reciprocal(cws[:, :, :], cws[:, :, :]))
            for k in range(2):
                nc.vector.tensor_tensor(lg[:, :, k, :], lg[:, :, k, :],
                                        cws[:, :, k].unsqueeze(2).broadcast_to([P, TT, E]), ALU.mult).then_inc(dve_step, 1)
                link.n += 1
            dve.wait_ge(dve_step, link.n)
            link(nc.vector.tensor_tensor(cw[:, :, :], lg[:, :, 0, :], lg[:, :, 1, :], ALU.mult))
            link(nc.vector.reduce_sum(cws[:, :, 0], cw[:, :, :], AX))
            link(nc.vector.tensor_scalar(cws[:, :, 0], cws[:, :, 0], 1e-9, None, ALU.add))
            link(nc.vector.reciprocal(cws[:, :, 1], cws[:, :, 0]))
            link(nc.vector.tensor_tensor(cw[:, :, :], cw[:, :, :],
                                         cws[:, :, 1].unsqueeze(2).broadcast_to([P, TT, E]), ALU.mult))
            link(nc.vector.tensor_copy(cwh[:, :, :], cw[:, :, :]))
            link(nc.vector.tensor_copy(cwhl[:, :, 0:E], cwh[:, :, :].bitcast(F32)))
            nc.vector.tensor_tensor(cwhl[:, :, E:2 * E], cw[:, :, :], cwh[:, :, :].bitcast(F32),
                                    ALU.subtract).then_inc(mix_ready, 1)

        HEAD_USES = ["ln2", "route", "mixT"]
        SSM_USES = ["ln1", "win", "dt"] + [f"{v}{k}" for k in range(KT) for v in "bc"] + ["proj"] + HEAD_USES
        UNITS = [(i, p) for i in range(NQT) for p in range(2)]
        ATT_USES = ["ln1"] + [f"{v}{g}" for g in range(4) for v in "qk"] + ["v0", "v1"]
        NUNIT = len(UNITS)
        for _n in range(NUNIT + 1):
            if _n < NUNIT:
                ATT_USES += [f"s{_n}.0", f"s{_n}.1"]
            if _n:
                ATT_USES += [f"t{_n - 1}.0", f"t{_n - 1}.1", f"o{_n - 1}"]

        def at(n):
            return 10 + (3 * n) // 2
        ATT_USES += ["attT", "proj"] + HEAD_USES

        def ssm_pe(pe, banks, slot):
            yield 2
            norm_pe(pe, banks, "ln1", 0)
            yield 4
            banks.take(pe, "win")
            banks.wait_free(pe, "ln1")
            banks.fill(nc.tensor.matmul(banks.ps("win")[:, :], pk("w_in"), sxT, start=True, stop=True), "win")
            yield 8
            pe.wait_ge(xs_done, 1)
            banks.take(pe, "dt")
            for v in range(2):
                last = nc.tensor.matmul(banks.ps("dt")[:, :], wdt[v][:, :], xs, start=v == 0, stop=v == 1)
            banks.fill(last, "dt")
            for k in range(KT):
                for w, name in ((0, f"b{k}"), (DSTATE, f"c{k}")):
                    yield 9 + 3 * k
                    banks.take(pe, name)
                    for v in range(2):
                        last = nc.tensor.matmul(banks.ps(name)[:, :],
                                                wbc[v][:, w + 2 * k:w + 2 * k + 2, :].rearrange("p a b -> p (a b)"),
                                                xs, start=v == 0, stop=v == 1)
                    banks.fill(last, name)
            yield 23
            banks.take(pe, "proj")
            pe.wait_ge(y_done, KT)
            for t in range(TT):
                ps = banks.ps("proj")[:, t * P:(t + 1) * P]
                nc.tensor.matmul(ps, tot[:, t * P:(t + 1) * P], pk("w_out_y"), start=True, stop=False)
                last = nc.tensor.matmul(ps, zb[0:INNER, t * P:(t + 1) * P], pk("w_out_z")[0:INNER, :],
                                        start=False, stop=True)
            banks.fill(last, "proj")
            yield 25
            for s in head_pe(pe, banks, slot, 1):
                yield 25 + s

        def ssm_act(act, link, banks, slot):
            yield 2
            banks.wait(act, "ln1")
            banks.free(nc.scalar.copy(sxT, banks.ps("ln1")[:, :]), "ln1")
            yield 5
            banks.wait_free(act, "win")
            nc.scalar.activation(xb2[0:INNER, :], cv[0:INNER, :], ACT.Silu).then_inc(silu_x, 1)
            nc.scalar.activation(xb2[INNER:P, :], cv[0:INNER, :], ACT.Silu).then_inc(silu_x, 1)
            act.wait_ge(silu_x, 2)
            nc.scalar.activation(xsm, xb2, ACT.Copy, scale=pk("lo_ssm")).then_inc(xs_m, 1)
            nc.scalar.activation(zb[0:INNER, :], cv[INNER:P, :], ACT.Silu).then_inc(silu_x, 1)
            for k in range(KT):
                yield 9 + 3 * k
                if k >= 1:
                    act.wait_ge(bx_done, k)
                    act.wait_ge(scan_done, k)
                banks.wait(act, f"b{k}")
                banks.free(nc.scalar.activation(btile, banks.ps(f"b{k}")[:, :], ACT.Tanh), f"b{k}")
                banks.wait_free(act, f"b{k}")
                if k >= 2:
                    act.wait_ge(y_done, k - 1)
                banks.wait(act, f"c{k}")
                banks.free(nc.scalar.activation(ctile[:, k % 2, :], banks.ps(f"c{k}")[:, :], ACT.Tanh, scale=-1.0), f"c{k}")
                if k == 0:
                    banks.wait_free(act, "dt")
                    link(nc.scalar.activation(delta, delta, ACT.Exp))
                    nc.scalar.activation(delta, delta, ACT.Ln, bias=1.0).then_inc(dt_soft, 1)
                    act.wait_ge(delta_done, 1)
                if k >= 2:
                    act.wait_ge(scan_done, k - 1)
                nc.scalar.activation(dec[:, k % 2, :], delta, ACT.Exp, scale=neg_a[:, k:k + 1]).then_inc(dec_exp, 1)
            yield 25
            for s in head_act(act, link, banks, slot):
                yield 25 + s

        def ssm_dve(dve, link, banks, slot, x_out, has_fin):
            if not has_fin:
                pass
            dve.wait_ge(loaded, 16)
            for s in norm_dve(dve, link, x_out, 0):
                yield s
            yield 4
            banks.wait(dve, "win")
            ps, kc = banks.ps("win"), pk("k_conv")
            link(nc.vector.tensor_scalar(cv, ps[:, :], kc[:, 1:2], None, ALU.mult))
            link(nc.vector.scalar_tensor_tensor(cv[:, 1:L], ps[:, 0:L - 1], kc[:, 0:1], cv[:, 1:L], ALU.mult, ALU.add))
            banks.free(nc.vector.scalar_tensor_tensor(cv[:, 0:L - 1], ps[:, 1:L], kc[:, 2:3], cv[:, 0:L - 1],
                                                      ALU.mult, ALU.add), "win")
            yield 6
            dve.wait_ge(xs_m, 1)
            nc.vector.tensor_tensor(xs, xb2, xsm.bitcast(F32), ALU.subtract).then_inc(xs_done, 1)
            yield 8
            banks.wait(dve, "dt")
            banks.free(nc.vector.tensor_scalar(delta, banks.ps("dt")[:, :], pk("b_dt"), 20.0, ALU.add, ALU.min), "dt")
            yield 9
            dve.wait_ge(dt_soft, 1)
            nc.vector.tensor_scalar(delta, delta, 1e-4, 1.0, ALU.max, ALU.min).then_inc(delta_done, 1)
            for k in range(KT):
                yield 11 + 3 * k
                dve.wait_ge(dec_exp, k + 1)
                link(nc.vector.tensor_scalar(dec[:, k % 2, :], dec[:, k % 2, :], 1e-4, 1.0, ALU.max, ALU.min))
                dve.wait_ge(bx_done, k + 1)
                link(nc.vector.scalar_tensor_tensor(btile, dec[:, k % 2, :], 1.0, btile, ALU.subtract, ALU.mult))
                nc.vector.tensor_tensor_scan(dec[:, k % 2, :], dec[:, k % 2, :], btile, 0.0, ALU.mult,
                                             ALU.add).then_inc(scan_done, 1)
                if k == 0:
                    yield 13
                    dve.wait_ge(y_part, 1)
                    nc.vector.scalar_tensor_tensor(tot, xb2, pk("d_skip"), ctile[:, 0, :], ALU.mult,
                                                   ALU.add).then_inc(y_done, 1)
            yield 23
            banks.wait(dve, "proj")
            banks.free(nc.vector.tensor_tensor(x_out[:, :, :].rearrange("p t d -> p (t d)"), banks.ps("proj")[:, :],
                                               x_out[:, :, :].rearrange("p t d -> p (t d)"), ALU.add), "proj")
            banks.wait_free(dve, "proj")
            for s in norm_dve(dve, link, x_out, 1):
                yield 23 + s
            yield 25
            for s in head_dve(dve, link, banks, slot, 1):
                yield 25 + s

        def ssm_pool(pool, link):
            norm_pool(pool, link, 0)
            for k in range(KT):
                yield 10 + 3 * k
                banks_b = SSM_BANKS[0]
                banks_b.wait_free(pool, f"b{k}")
                nc.gpsimd.tensor_tensor(btile, btile, xb2, ALU.mult).then_inc(bx_done, 1)
                yield 12 + 3 * k
                banks_b.wait_free(pool, f"c{k}")
                pool.wait_ge(scan_done, k + 1)
                c = ctile[:, k % 2, :]
                if k == 0:
                    nc.gpsimd.tensor_tensor(c, c, dec[:, 0, :], ALU.mult).then_inc(y_part, 1)
                else:
                    link(nc.gpsimd.tensor_tensor(c, c, dec[:, k % 2, :], ALU.mult))
                    pool.wait_ge(y_done, k)
                    nc.gpsimd.tensor_tensor(tot, tot, c, ALU.add).then_inc(y_done, 1)
            yield 23
            norm_pool(pool, link, 1)

        SSM_BANKS = [None]

        def size(i):
            nq = min(QT, L - i * QT)
            left = LEFT if i else 0
            return nq, nq + left, i * QT - left, LEFT - left

        def att_pe(pe, banks, slot):
            yield 3
            norm_pe(pe, banks, "ln1", 0)
            for g in range(4):
                yield 5 + g
                pe.wait_ge(x_hi, 1)
                pe.wait_ge(x_lo, 1)
                for w, name in ((wq, f"q{g}"), (wk, f"k{g}")):
                    banks.take(pe, name)
                    wa = [w[v][:, g, :, :, :].rearrange("p a b c -> p (a b c)") for v in range(2)]
                    banks.fill(split3(banks.ps(name)[:, :], wa, (axh[:, 0:L], axl[:, 0:L])), name)
            for half_v in range(2):
                yield 9
                name = f"v{half_v}"
                banks.take(pe, name)
                for i in range(4 * half_v, min(NQT, 4 * half_v + 4)):
                    nk = size(i)[1]
                    out = banks.ps(name)[0:nk, (i % 4) * P:(i % 4 + 1) * P]
                    k0 = size(i)[2]
                    xw = [a[:, k0:k0 + nk] for a in (axh, axl)]
                    nc.tensor.matmul(out, xw[0], wv[0][:, :], start=True, stop=False)
                    nc.tensor.matmul(out, xw[1], wv[0][:, :], start=False, stop=False)
                    last = nc.tensor.matmul(out, xw[0], wv[1][:, :], start=False, stop=True)
                banks.fill(last, name)

            def scores(n):
                i, p = UNITS[n]
                nq, nk, k0, m0 = size(i)
                for rr in range(2):
                    r, name = 2 * p + rr, f"s{n}.{rr}"
                    banks.take(pe, name)
                    for g in range(4):
                        nke = nk + nk % 2
                        last = nc.tensor.matmul(banks.ps(name)[0:nq, g * KW:g * KW + nke],
                                                q3[32 * r:32 * r + 32, g, i * QT:i * QT + nq],
                                                k3[32 * r:32 * r + 32, g, k0:k0 + nke], start=True, stop=True)
                    banks.fill(last, name)

            def values(n):
                i, p = UNITS[n]
                nq, nk, k0, m0 = size(i)
                name = f"o{n}"
                banks.take(pe, name)
                banks.wait_free(pe, f"t{n}.0")
                banks.wait_free(pe, f"t{n}.1")
                if p == 0 and i == 0:
                    banks.wait_free(pe, "v1")
                for rr in range(2):
                    for g in range(4):
                        h = 4 * g + 2 * p + rr
                        last = nc.tensor.matmul(banks.ps(name)[0:nq, (rr * 4 + g) * 9:(rr * 4 + g + 1) * 9],
                                                pt_u[0:nk, rr, g, 0:nq], v_t[0:nk, i, h, :], start=True, stop=True)
                banks.fill(last, name)

            banks.wait_free(pe, "q3")
            banks.wait_free(pe, "k3")
            yield at(0)
            scores(0)
            for n in range(NUNIT):
                i, p = UNITS[n]
                nq, nk, k0, m0 = size(i)
                if n + 1 < NUNIT:
                    yield at(n + 1)
                    scores(n + 1)
                yield at(n) + 2
                pe.wait_ge(s_exp, n + 1)
                for rr in range(2):
                    name = f"t{n}.{rr}"
                    banks.take(pe, name)
                    for g in range(4):
                        last = nc.tensor.transpose(banks.ps(name)[0:nk, g * QT:g * QT + nq],
                                                   s_u[n % 2][0:nq, rr, g, 0:nk], ident[0:nq, 0:nq])
                    banks.fill(last, name)
                yield at(n) + 3
                values(n)
            yield 29
            banks.take(pe, "attT")
            banks.wait_free(pe, f"o{len(UNITS) - 1}")
            for i in range(NQT):
                nq = size(i)[0]
                last = nc.tensor.transpose(banks.ps("attT")[:, i * QT:i * QT + nq], att[0:nq, i, :], ident[0:nq, 0:nq])
            banks.fill(last, "attT")
            yield 30
            banks.take(pe, "proj")
            banks.wait_free(pe, "attT")
            for t in range(TT):
                last = nc.tensor.matmul(banks.ps("proj")[:, t * P:(t + 1) * P], attT[:, t * P:(t + 1) * P], pk("w_o"),
                                        start=True, stop=True)
            banks.fill(last, "proj")
            yield 31
            for s in head_pe(pe, banks, slot, 1):
                yield 31 + s

        def att_act(act, link, banks, slot):
            yield 3
            banks.wait(act, "ln1")
            nc.scalar.copy(axh[:, 0:L], banks.ps("ln1")[:, :]).then_inc(x_hi, 1)
            for g in range(4):
                yield 5 + g
                for j, v in enumerate("qk"):
                    banks.wait(act, f"{v}{g}")
                    dst = q3[:, g, :] if v == "q" else k3[:, g, 0:L]
                    nc.scalar.activation(dst, banks.ps(f"{v}{g}")[:, :], ACT.Identity,
                                         bias=bq_lo[:, 4 * j + g:4 * j + g + 1], scale=pk("lo_" + v)).then_inc(q_lo_m, 1)
            for n in range(len(UNITS)):
                i, p = UNITS[n]
                nq, nk, k0, m0 = size(i)
                yield at(n) + 1
                act.wait_ge(s_sub, n + 1)
                u = s_u[n % 2][0:nq, :, :, 0:nk]
                nc.scalar.activation(u, u, ACT.Exp, scale=float(HD) ** -0.5).then_inc(s_exp, 1)
                yield at(n) + 2
                if n >= 1:
                    banks.wait(act, f"o{n - 1}")
                for rr in range(2):
                    banks.wait(act, f"t{n}.{rr}")
                    banks.free(nc.scalar.copy(pt_u[0:nk, rr, :, 0:nq],
                                              banks.ps(f"t{n}.{rr}")[0:nk, 0:4 * QT].rearrange("p (g q) -> p g q", g=4)[:, :, 0:nq]),
                               f"t{n}.{rr}")
            yield 29
            banks.wait(act, "attT")
            banks.free(nc.scalar.copy(attT, banks.ps("attT")[:, :]), "attT")
            yield 31
            for s in head_act(act, link, banks, slot):
                yield 31 + s

        def att_dve(dve, link, banks, slot, x_out):
            for s in norm_dve(dve, link, x2, 0):
                yield s
            yield 3
            dve.wait_ge(x_hi, 1)
            banks.free(nc.vector.tensor_tensor(axl[:, 0:L], banks.ps("ln1")[:, :],
                                               axh[:, 0:L].bitcast(F32), ALU.subtract), "ln1")
            banks.wait_free(dve, "ln1")
            nc.vector.memset(v_t[:, :, :, HD:HD + 1], 1.0).then_inc(x_lo, 1)
            dve.wait_ge(x_lo, 1)
            for g in range(4):
                yield 5 + g
                for j, v in enumerate("qk"):
                    dve.wait_ge(q_lo_m, 2 * g + j + 1)
                    dst = q3[:, g, :] if v == "q" else k3[:, g, 0:L]
                    banks.free(nc.vector.scalar_tensor_tensor(dst, banks.ps(f"{v}{g}")[:, :], pk("b_" + v)[:, g:g + 1],
                                                              dst.bitcast(F32), ALU.add, ALU.subtract), f"{v}{g}")
            yield 9
            for half_v in range(2):
                banks.wait(dve, f"v{half_v}")
                lo, hi = 4 * half_v, min(NQT, 4 * half_v + 4)
                for i in range(lo, hi):
                    nk = size(i)[1]
                    ins = nc.vector.tensor_tensor(
                        v_t[0:nk, i, :, 0:HD],
                        banks.ps(f"v{half_v}")[0:nk, (i % 4) * P:(i % 4 + 1) * P].rearrange("p (h e) -> p h e", e=HD),
                        pk("b_v")[0:nk, :].rearrange("p (h e) -> p h e", e=HD), ALU.add)
                    if i == hi - 1:
                        banks.free(ins, f"v{half_v}")
                    else:
                        link(ins)
            def masked(n):
                i, p = UNITS[n]
                nq, nk, k0, m0 = size(i)
                mask = pk("mask")[:, m0:m0 + nk]
                if n >= 2:
                    banks.wait(dve, f"t{n - 2}.1")
                for rr in range(2):
                    banks.wait(dve, f"s{n}.{rr}")
                    ps = banks.ps(f"s{n}.{rr}")[0:nq, 0:4 * KW].rearrange("p (g k) -> p g k", g=4)[:, :, 0:nk]
                    banks.free(nc.vector.tensor_tensor(s_u[n % 2][0:nq, rr, :, 0:nk], ps,
                                                       mask[0:nq, :].unsqueeze(1).broadcast_to([nq, 4, nk]), ALU.add),
                               f"s{n}.{rr}")
                banks.wait_free(dve, f"s{n}.0")
                banks.wait_free(dve, f"s{n}.1")
                if n >= 1:
                    dve.wait_ge(s_sub, n)
                nc.vector.reduce_max(smax[0:nq, :, :], s_u[n % 2][0:nq, :, :, 0:nk], AX).then_inc(s_max, 1)

            def normalised(n):
                i, p = UNITS[n]
                nq = size(i)[0]
                banks.wait(dve, f"o{n}")
                ps = banks.ps(f"o{n}")[0:nq, 0:72].rearrange("p (r g e) -> p r g e", r=2, g=4)
                link(nc.vector.reciprocal(rinv[0:nq, :, :], ps[:, :, :, HD]))
                banks.free(nc.vector.tensor_tensor(
                    att[0:nq, i, :].rearrange("p (g r e) -> p r g e", g=4, r=4)[:, 2 * p:2 * p + 2, :, :],
                    ps[:, :, :, 0:HD], rinv[0:nq, :, :].unsqueeze(3).broadcast_to([nq, 2, 4, HD]), ALU.mult), f"o{n}")

            yield at(0)
            masked(0)
            for n in range(NUNIT):
                if n + 1 < NUNIT:
                    yield at(n + 1)
                    masked(n + 1)
                yield at(n) + 3
                normalised(n)
            yield 30
            banks.wait(dve, "proj")
            dve.wait_ge(x3_pre, 1)
            if x_out is x3:
                dve.wait_ge(stored, 16 * stores_before[0])
            xo = x_out[:, :, :].rearrange("p t d -> p (t d)")
            banks.free(nc.vector.tensor_tensor(xo, banks.ps("proj")[:, :],
                                               x2[:, :, :].rearrange("p t d -> p (t d)"), ALU.add), "proj")
            banks.wait_free(dve, "proj")
            for s in norm_dve(dve, link, x_out, 1):
                yield 30 + s
            yield 31
            for s in head_dve(dve, link, banks, slot, 2):
                yield 31 + s

        stores_before = [0]

        def att_pool(pool, link):
            norm_pool(pool, link, 0)
            yield 2
            pool.wait_ge(ln_out, TT)
            nc.gpsimd.tensor_tensor(x2[:, :, :], x2[:, :, :], pk("b_o").unsqueeze(1).broadcast_to([P, TT, D]),
                                    ALU.add).then_inc(x3_pre, 1)
            for n in range(len(UNITS)):
                i, p = UNITS[n]
                nq, nk, k0, m0 = size(i)
                yield at(n)
                pool.wait_ge(s_max, n + 1)
                for rr in range(2):
                    u = s_u[n % 2][0:nq, rr, :, 0:nk]
                    ins = nc.gpsimd.tensor_tensor(u, u, smax[0:nq, rr, :].unsqueeze(2).broadcast_to([nq, 4, nk]), ALU.subtract)
                    if rr == 0:
                        ins.then_inc(pool_step, 1)
                        link.n += 1
                    else:
                        pool.wait_ge(pool_step, link.n)
                        ins.then_inc(s_sub, 1)
            yield 30
            norm_pool(pool, link, 1)

        def phase(main=None, side=None, slot=0, x_out=None, fin=None, load=None, store=None, setup=False):
            banks = Banks((["fin"] if fin else []) + {"ssm": SSM_USES, "att": ATT_USES, None: []}[side])
            SSM_BANKS[0] = banks
            stores_before[0] = 1 if store is not None else 0

            def run(gen, c):
                while run_at[0] is not None and run_at[0] <= c:
                    run_at[0] = next(gen, None)

            def interleave(gen, steps):
                run_at[0] = 0
                for c, step in enumerate(steps):
                    step()
                    run(gen, c)
                run(gen, 10 ** 6)

            def w_part(j, v):
                return (wg, wu, wd)[j // E][v][:, CPE * (j % E):CPE * (j % E + 1), :].rearrange("p a b -> p (a b)")

            run_at = [0]
            nslots = NCH + LAG
            with nc.Block() as block:

                @block.sync
                def _(sp):
                    if setup:
                        sp.dma_start(raw, pack_d[:, 0:NRAW]).then_inc(packed, 16)
                        sp.dma_start(pack[:, :], pack_d[:, NRAW:NPACK]).then_inc(packed, 16)
                    if load is not None:
                        if fin:
                            banks.wait_free(sp, "fin")
                        sp.dma_start(x_out[:, :, :], x_d[load].rearrange("(t p) d -> p t d", p=P)).then_inc(loaded, 16)
                    if setup:
                        for j in range(3 * E):
                            if j >= 3:
                                sp.wait_ge(w_lo, j - 2)
                            dst, src = h_b[:, j % 3, :], (wg_d, wu_d, wd_d)[j // E][j % E]
                            if j >= 2 * E:
                                src = src.rearrange("(c p) h -> p c h", p=P)
                                dst = dst.rearrange("p (c h) -> p c h", h=P)
                            sp.dma_start(dst, src).then_inc(w_loaded[j % 3], 16)
                    if store is not None:
                        banks.wait_free(sp, "fin")
                        sp.dma_start(out_d[store].rearrange("(t p) d -> p t d", p=P), fin[1][:, :, :]).then_inc(stored, 16)
                        sp.wait_ge(stored, 16)

                @block.tensor
                def _(pe):
                    def chunk(c):
                        xh, xl = fxh[main][:, :], fxl[main][:, :]
                        if c == 0:
                            mix(0)
                        if c < NCH:
                            e = c // CPE
                            if c >= 2:
                                pe.wait_ge(silu_done, c - 1)
                            split3(pg[c % 2][:, :], [w[:, c, :] for w in wg], (xh, xl)).then_inc(g_full, 1)
                            if c >= 2:
                                pe.wait_ge(h_done, c - 1)
                            if c % CPE == 0:
                                pe.wait_ge(xel_done, e + 1)
                            split3(pu[c % 2][:, :], [w[:, c, :] for w in wu],
                                   (xeh[:, e % 2, :], xel[:, e % 2, :])).then_inc(u_full, 1)
                            if c % CPE == 1 and e + 1 < E:
                                mix(e + 1)
                        d = c - LAG
                        if d >= 0:
                            pe.wait_ge(hl_done, d + 1)
                            split3(pd[:, :], [w[:, d, :] for w in wd], (hh_b[:, d % 3, :], hl_b[:, d % 3, :]),
                                   first=d == 0, last=d == NCH - 1).then_inc(down_done, 1)

                    def mix(e):
                        if e >= 1:
                            pe.wait_ge(xe_done, e)
                        nc.tensor.matmul(pb[:, :], sel[32 * main:32 * main + 2 * E, e:e + 1].broadcast_to([2 * E, P]), cwT[main], start=True, stop=True).then_inc(mix_full, 1)

                    def side_pe():
                        if fin:
                            finish_pe(pe, banks)
                            yield 0
                        if side == "ssm":
                            yield from ssm_pe(pe, banks, slot)
                        if side == "att":
                            yield from att_pe(pe, banks, slot)

                    if setup:
                        pe.wait_ge(packed, 32)
                        nc.tensor.matmul(pg[0][:, 0:P], pk("w_dtx")[0:DTRANK, :], pk("w_dt")[0:DTRANK, :],
                                         start=True, stop=True).then_inc(g_full, 1)
                        pe.wait_ge(w_small, 1)
                    steps = [lambda c=c: chunk(c) for c in range(nslots)] if main is not None else []
                    interleave(side_pe(), steps)

                @block.scalar
                def _(act):
                    link = Chain(act, act_step)

                    def chunk(c):
                        if c < NCH:
                            act.wait_ge(g_full, c + 1)
                            if c >= 3:
                                act.wait_ge(hl_done, c - 2)
                            nc.scalar.activation(h_b[:, c % 3, :], pg[c % 2][:, :], ACT.Silu).then_inc(silu_done, 1)

                    def split_w(j):
                        act.wait_ge(w_loaded[j % 3], 16 * (j // 3 + 1))
                        nc.scalar.copy(w_part(j, 0), h_b[:, j % 3, :]).then_inc(w_hi, 1)

                    def side_act():
                        if side == "ssm":
                            yield from ssm_act(act, link, banks, slot)
                        if side == "att":
                            yield from att_act(act, link, banks, slot)

                    if setup:
                        act.wait_ge(w_prep, 1)
                        link(nc.scalar.activation(neg_a[:, :], neg_a[:, :], ACT.Exp, scale=-1.0))
                        nc.scalar.activation(neg_a[:, :], neg_a[:, :], ACT.Ln, bias=1.0).then_inc(w_prep, 1)
                        interleave(side_act(), [lambda j=j: split_w(j) for j in range(3 * E)])
                    else:
                        interleave(side_act(), [lambda c=c: chunk(c) for c in range(nslots)] if main is not None else [])
                        if main is not None:
                            act.wait_ge(down_done, NCH)
                            if fin:
                                banks.wait(act, "fin")
                            nc.scalar.copy(ffn_out[:, :], pd[:, :]).then_inc(ffn_ready, 1)

                @block.vector
                def _(dve):
                    link = Chain(dve, dve_step)

                    def expert_in(e):
                        dve.wait_ge(mix_full, e + 1)
                        if e >= 1:
                            dve.wait_ge(xel_done, e)
                        if e >= 2:
                            dve.wait_ge(u_full, CPE * (e - 1))
                        nc.vector.tensor_tensor(xe[:, :], pb[:, :], fx[main][:, :], ALU.mult).then_inc(xe_done, 1)
                        dve.wait_ge(xe_done, e + 1)
                        nc.vector.tensor_copy(xeh[:, e % 2, :], xe[:, :]).then_inc(xeh_done, 1)

                    def chunk(c):
                        if c == 0:
                            expert_in(0)
                        if c < NCH:
                            dve.wait_ge(silu_done, c + 1)
                            dve.wait_ge(u_full, c + 1)
                            nc.vector.tensor_tensor(h_b[:, c % 3, :], pu[c % 2][:, :], h_b[:, c % 3, :],
                                                    ALU.mult).then_inc(h_done, 1)
                            dve.wait_ge(h_done, c + 1)
                            if c >= 3:
                                dve.wait_ge(down_done, c - 2)
                            nc.vector.tensor_copy(hh_b[:, c % 3, :], h_b[:, c % 3, :]).then_inc(hh_done, 1)
                            if c % CPE == 1 and c // CPE + 1 < E:
                                expert_in(c // CPE + 1)

                    def split_w(j):
                        dve.wait_ge(w_hi, j + 1)
                        nc.vector.tensor_tensor(w_part(j, 1), h_b[:, j % 3, :], w_part(j, 0).bitcast(F32),
                                                ALU.subtract).then_inc(w_lo, 1)

                    def side_dve():
                        if fin:
                            finish_dve(dve, link, banks, *fin)
                            yield 0
                        if side == "ssm":
                            yield from ssm_dve(dve, link, banks, slot, x_out, fin)
                        if side == "att":
                            yield from att_dve(dve, link, banks, slot, x_out)

                    def small_weights():
                        def both(dst, src):
                            link(nc.vector.tensor_copy(dst[0], src))
                            link(nc.vector.tensor_tensor(dst[1], src, dst[0].bitcast(F32), ALU.subtract))

                        dve.wait_ge(packed, 32)
                        link(nc.vector.tensor_scalar(mv[:, 0:TT, 0], pk("a_log"), -1.0, None, ALU.mult))
                        nc.vector.tensor_tensor(neg_a[:, :], mv[:, 0:TT, 0], pk("a_log"), ALU.max).then_inc(w_prep, 1)
                        for w, name in ((wq, "w_q"), (wk, "w_k")):
                            src = pk(name).rearrange("p (g h e) -> p g h e", g=4, h=4)
                            for g in range(4):
                                both([v[:, g, :, :, :] for v in w],
                                     src[:, g, :, :].unsqueeze(2).broadcast_to([P, 4, 4, HD]))
                        both([w[:, :] for w in wv], pk("w_v"))
                        both([w[:, :, :] for w in wbc], pk("w_bc").unsqueeze(2).broadcast_to([P, 2 * DSTATE, INNER]))
                        link(nc.vector.tensor_copy(sel[:, :], pk("sel")[0:32 + 2 * E, :]))
                        dve.wait_ge(g_full, 1)
                        link(nc.vector.tensor_copy(xe[:, 0:P], pg[0][:, 0:P]))
                        both([w[:, :] for w in wdt], xe[:, 0:P])
                        for j, v in enumerate("qk"):
                            link(nc.vector.tensor_scalar(bq_lo[:, 4 * j:4 * j + 4], pk("b_" + v), pk("lo_" + v), None, ALU.mult))
                        dve.wait_ge(w_prep, 2)
                        link(nc.vector.scalar_tensor_tensor(neg_a[:, :], pk("a_log"), 0.0, neg_a[:, :], ALU.max, ALU.add))
                        nc.vector.tensor_scalar(neg_a[:, :], neg_a[:, :], -1.0, -1e-4, ALU.mult, ALU.add).then_inc(w_small, 1)
                        dve.wait_ge(w_small, 1)

                    if setup:
                        small_weights()
                        interleave(side_dve(), [lambda j=j: split_w(j) for j in range(3 * E)])
                    else:
                        interleave(side_dve(), [lambda c=c: chunk(c) for c in range(nslots)] if main is not None else [])

                @block.gpsimd
                def _(pool):
                    link = Chain(pool, pool_step)

                    def chunk(c):
                        e = c // CPE
                        if c % CPE == 0 and c < NCH:
                            pool.wait_ge(xeh_done, e + 1)
                            nc.gpsimd.tensor_tensor(xel[:, e % 2, :], xe[:, :], xeh[:, e % 2, :].bitcast(F32),
                                                    ALU.subtract).then_inc(xel_done, 1)
                        d = c
                        if d < NCH:
                            pool.wait_ge(hh_done, d + 1)
                            nc.gpsimd.tensor_tensor(hl_b[:, d % 3, :], h_b[:, d % 3, :], hh_b[:, d % 3, :].bitcast(F32),
                                                    ALU.subtract).then_inc(hl_done, 1)

                    def side_pool():
                        if side == "ssm":
                            yield from ssm_pool(pool, link)
                        if side == "att":
                            yield from att_pool(pool, link)

                    if setup:
                        link(nc.gpsimd.memset(half[:, :], -0.5))
                        for buf in (axh[:, L:XW], axl[:, L:XW], k3[:, :, L:XW]):
                            link(nc.gpsimd.memset(buf.bitcast(F32), 0.0))
                    interleave(side_pool(), [lambda c=c: chunk(c) for c in range(nslots)] if main is not None else [])

            nc.all_engine_barrier()
            nums = sorted(s.num for s in sems)
            nc.gpsimd.sem_clear(range(nums[0], nums[-1] + 1))
            nc.all_engine_barrier()

        phase(setup=True, side="ssm", slot=0, x_out=x2, load=0)
        phase(main=0, side="ssm", slot=1, x_out=x1, load=1)
        phase(main=1, side="att", slot=0, x_out=x3, fin=(x2, x2))
        with nc.Fori(1, B - 1) as j:
            phase(main=0, side="ssm", slot=1, x_out=x1, fin=(x1, x2), load=j + 1)
            phase(main=1, side="att", slot=0, x_out=x3, fin=(x3, x3), store=j - 1)
        phase(main=0, side="att", slot=1, x_out=x1, fin=(x1, x2))
        phase(main=1, fin=(x3, x3), store=B - 2)
        phase(fin=(x1, x1), store=B - 1)


def _pack(w):
    out = np.zeros((P, NPACK), np.float32)

    def put(name, a):
        at, n = _COLS[name]
        a = np.asarray(a)
        out[:a.shape[0], at:at + a.shape[1]] = a

    a_ = "L0_attn_a_"
    b_ = "L0_attn_b_"
    w_x = w[a_ + "W_xproj"]
    put("w_in", w[a_ + "W_in"].T)
    put("w_bc", np.concatenate([w_x[DTRANK:].T] * 2, 0))
    put("w_dtx", np.concatenate([w_x[:DTRANK]] * 2, 1))
    put("w_dt", np.concatenate([w[a_ + "W_dt"].T] * 2, 1))
    put("k_conv", np.concatenate([w[a_ + "Kx"][:, 0, :], w[a_ + "Kz"][:, 0, :]], 0))
    put("b_dt", np.concatenate([w[a_ + "b_dt"]] * 2)[:, None])
    put("a_log", w[a_ + "A_log"].reshape(INNER, KT, 2).transpose(2, 0, 1).reshape(P, KT))
    put("d_skip", w[a_ + "D"][:, None])
    w_out = w[a_ + "W_out"].T
    put("w_out_y", np.concatenate([w_out[:INNER]] * 2, 0))
    put("w_out_z", w_out[INNER:])
    put("w_route", np.concatenate([w["L0_ffn_w_router"], w["L0_ffn_w_gating"]], 1))
    put("w_q", w[b_ + "Wq"].T)
    put("w_k", w[b_ + "Wk"].T)
    for v in "qk":
        put("b_" + v, np.repeat(w[b_ + "b" + v].reshape(4, 4, 1, HD), 4, 2).reshape(4, P).T)
    put("w_v", w[b_ + "Wv"].T)
    put("b_v", np.repeat(w[b_ + "bv"][None, :], P, 0))
    put("w_o", w[b_ + "Wo"].T)
    put("b_o", np.repeat(w[b_ + "bo"][None, :], P, 0))
    put("ident", np.eye(P))
    q, k = np.arange(QT)[:, None], np.arange(KW)[None, :]
    ok = (k >= q) & (k - LEFT < (q // CHUNK + 1) * CHUNK)
    put("mask", np.where(ok, 0.0, NEG))
    put("sel", np.concatenate([np.eye(E)] * 6, 0))
    put("lo_ssm", (np.arange(P) >= INNER)[:, None])
    copy = np.arange(P) // HD % 4
    put("lo_q", (copy >= 2)[:, None])
    put("lo_k", (copy % 2 == 1)[:, None])
    return out


def kernel(**inputs):
    import concourse.bacc as bacc
    from concourse.bass_utils import run_bass_kernel_spmd as run

    w = {k: np.asarray(v) for k, v in inputs.items()}
    arrays = {"x": w["L0_attn_a_x"], "pack": _pack(w), "w_gate": w["L0_ffn_w_gate"],
              "w_up": w["L0_ffn_w_up"], "w_down": w["L0_ffn_w_down"]}
    nc = bacc.Bacc("TRN2", target_bir_lowering=False, num_devices=1)
    aps = [nc.dram_tensor("in_" + n, a.shape, F32, kind="ExternalInput").ap() for n, a in arrays.items()]
    out = nc.dram_tensor("out", (B, L, D), F32, kind="ExternalOutput").ap()
    build(nc, *aps, out)
    r = run(nc, [{"in_" + n: np.ascontiguousarray(a) for n, a in arrays.items()}], core_ids=[0])
    return r.results[0]["out"]
```

```python
import contextlib

import numpy as np

import concourse.bass as bass
from concourse import mybir
from concourse.alu_op_type import AluOpType as ALU

F32 = mybir.dt.float32
F32R = mybir.dt.float32r
ACT = mybir.ActivationFunctionType
AX = mybir.AxisListType.X

B, L, D = 8, 512, 128
P = 128
TT = L // P
INNER, DSTATE, DTRANK = 64, 8, 8
KT = INNER * DSTATE // P
HEADS, HD = 16, 8
CHUNK, LEFT = 10, 25
QT = 100
NQT = -(-L // QT)
KW = QT + LEFT + 1
E, F = 8, 512
NCH = E * F // P
CPE = F // P
LAG = 4
HH_SSM, HH_ATT = (0, 1, 2, 3), (0, 1, 2, 3)
EDGE_PACE = 1.25
FORM_SSM, FORM_ATT = "tanh", "tanh"
EPS = 1e-5
NEG = -1e30

_COLS = {}


def _layout():
    at = 0
    for name, n in (("w_bc", 16), ("w_dtx", 128), ("w_dt", 128), ("w_q", 128), ("w_k", 128), ("w_v", 128),
                    ("w_in", 128), ("k_conv", 3),
                    ("b_dt", 1), ("a_log", KT), ("d_skip", 1), ("w_out_y", 128), ("w_out_z", 128),
                    ("w_route", 2 * E), ("b_q", 4), ("b_k", 4),
                    ("b_v", 128), ("w_o", 128), ("b_o", 128), ("ident", 128),
                    ("mask", KW), ("sel", E), ("lo_ssm", 1), ("lo_q", 1),
                    ("lo_k", 1)):
        _COLS[name] = (at, n)
        at += n
    return at


NPACK = _layout()
NRAW = _COLS["w_in"][0]


def build(nc, x_d, pack_d, wg_d, wu_d, wd_d, out_d):
    ctx = contextlib.ExitStack()
    with ctx:
        def sb(name, shape, dt=F32):
            return ctx.enter_context(nc.sbuf_tensor(name, shape, dt))

        def sem(name):
            s = ctx.enter_context(nc.semaphore(name))
            sems.append(s)
            return s

        sems = []
        pack = sb("pack", [P, NPACK - NRAW])

        def pk(name):
            at, n = _COLS[name]
            return pack[:, at - NRAW:at - NRAW + n] if at >= NRAW else raw[:, at:at + n]

        sel = sb("sel", [32 + 2 * E, E], F32R)
        wg = [sb(f"w_gate_{v}", [P, NCH, P], F32R) for v in ("hi", "lo")]
        wu = [sb(f"w_up_{v}", [P, NCH, P], F32R) for v in ("hi", "lo")]
        wd = [sb(f"w_down_{v}", [P, NCH, P], F32R) for v in ("hi", "lo")]
        wq = [sb(f"w_q_{v}", [P, 4, 4, 4, HD], F32R) for v in ("hi", "lo")]
        wk = [sb(f"w_k_{v}", [P, 4, 4, 4, HD], F32R) for v in ("hi", "lo")]
        wv = [sb(f"w_v_{v}", [P, P], F32R) for v in ("hi", "lo")]
        wbc = [sb(f"w_bc_{v}", [P, 2 * DSTATE, INNER], F32R) for v in ("hi", "lo")]
        wdt = [sb(f"w_dt_{v}", [P, P], F32R) for v in ("hi", "lo")]
        neg_a = sb("neg_a", [P, KT])
        bq_lo = sb("bq_lo", [P, 8])
        half = sb("half", [P, TT])

        x1 = sb("x1", [P, TT, D])
        x2 = sb("x2", [P, TT, D])
        x3 = sb("x3", [P, TT, D])
        ffn_out = sb("ffn_out", [P, L])

        fx = [sb(f"ffn_x{s}", [P, L]) for s in range(2)]
        fxh = [sb(f"ffn_x_hi{s}", [P, L], F32R) for s in range(2)]
        fxl = [sb(f"ffn_x_lo{s}", [P, L], F32R) for s in range(2)]
        mixT = sb("mix_t", [32 + 2 * E, L], F32R)
        cwT = [mixT[32 * s:32 * s + 2 * E, :] for s in range(2)]

        h_b = sb("h", [P, 3, L])
        hh_b = sb("h_hi", [P, 3, L], F32R)
        hl_b = sb("h_lo", [P, 3, L], F32R)
        xe = sb("xe", [P, L])
        xeh = sb("xe_hi", [P, 2, L], F32R)
        xel = sb("xe_lo", [P, 2, L], F32R)

        bn6 = sb("bn6", [P, TT, 6])
        mv = sb("mv", [P, TT, 2])
        rstd = sb("rstd", [P, TT])
        lg = sb("route", [P, TT, 2, E])
        lmax = sb("route_max", [P, TT, 2])
        cw = sb("mix", [P, TT, E])
        cws = sb("mix_sums", [P, TT, 2])
        cwh = sb("mix_hi", [P, TT, E], F32R)
        cwhl = sb("mix_hi_lo", [P, TT, 2 * E])
        arena = sb("arena", [P, 9, L])
        xb2, zb, delta, tot, cv, sxT = (arena[:, i, :] for i in range(6))
        btile, ctile = arena[:, 6, :], arena[:, 7:9, :]
        dec = arena[:, 4:6, :]
        xn = arena[:, 0, :].rearrange("p (t d) -> p t d", t=TT)
        flat = arena[:, :, :].rearrange("p a b -> p (a b)")
        raw = flat[:, 7 * L:7 * L + NRAW]
        NU = 8 * KW
        s_u = [flat[:, i * NU:(i + 1) * NU].rearrange("p (r g k) -> p r g k", r=2, g=4) for i in range(2)]
        pt_u = flat[:, 2 * NU:2 * NU + 8 * QT].rearrange("p (r g q) -> p r g q", r=2, g=4)
        o1 = 2 * NU + 8 * QT
        v_t = flat[:, o1:o1 + NQT * HEADS * 9].rearrange("p (t h e) -> p t h e", t=NQT, e=9)
        o1 += NQT * HEADS * 9
        att = flat[:, o1:o1 + NQT * D].rearrange("p (t e) -> p t e", t=NQT)
        o1 += NQT * D
        attT = flat[:, 0:L]
        smax = flat[:, o1:o1 + 8].rearrange("p (r g) -> p r g", r=2)
        rinv = flat[:, o1 + 8:o1 + 16].rearrange("p (r g) -> p r g", r=2)
        assert o1 + 16 <= 9 * L
        XW = L + 2
        axh = sb("attn_x_hi", [P, XW], F32R)
        axl = sb("attn_x_lo", [P, XW], F32R)
        q3 = sb("q3", [P, 4, L], F32R)
        k3 = sb("k3", [P, 4, XW], F32R)
        xs = axl[:, 0:L]
        xsm = axh[:, 0:L]

        pg = [ctx.enter_context(nc.psum_tensor(f"pg{i}", [P, L], F32)) for i in range(3)]
        pu = [ctx.enter_context(nc.psum_tensor(f"pu{i}", [P, L], F32)) for i in range(2)]
        pd = ctx.enter_context(nc.psum_tensor("pd", [P, L], F32))
        side_ps = [ctx.enter_context(nc.psum_tensor(f"ps{i}", [P, L], F32)) for i in range(2)]

        packed, raw_loaded, res_loaded, stored = sem("packed"), sem("raw_loaded"), sem("res_loaded"), sem("stored")
        w_loaded = [sem(f"w_loaded{i}") for i in range(3)]
        w_hi, w_lo, w_small, w_prep, wdt_full = sem("w_hi"), sem("w_lo"), sem("w_small"), sem("w_prep"), sem("wdt_full")
        g_full, u_full, gate_done, h_done = sem("g_full"), sem("u_full"), sem("gate_done"), sem("h_done")
        gated = sem("gated")
        hh_done = {"act": sem("hh_act"), "dve": sem("hh_dve")}
        hl_done, down_done, ffn_ready = sem("hl_done"), sem("down_done"), sem("ffn_ready")
        mix_full, xe_done, xeh_done, xel_done = sem("mix_full"), sem("xe_done"), sem("xeh_done"), sem("xel_done")
        bank_full = [sem("bank_full0"), sem("bank_full1")]
        bank_free = [sem("bank_free0"), sem("bank_free1")]
        ln_sems = {k: (sem(f"{k}_stats"), sem(f"{k}_rstd"), sem(f"{k}_rows")) for k in ("ssm_ln", "att_ln", "ffn_ln")}
        fx_hi, fx_f32, route_exp, mix_ready = sem("fx_hi"), sem("fx_f32"), sem("route_exp"), sem("mix_ready")
        silu_x, xs_m, xs_done = sem("silu_x"), sem("xs_m"), sem("xs_done")
        dt_soft, delta_done = sem("dt_soft"), sem("delta_done")
        bx_done, dec_exp, scan_done = sem("bx_done"), sem("dec_exp"), sem("scan_done")
        y_part, y_done = sem("y_part"), sem("y_done")
        x_hi, q_lo_m = sem("x_hi"), sem("q_lo_m")
        s_max, s_sub, s_exp, x2_bias = sem("s_max"), sem("s_sub"), sem("s_exp"), sem("x2_bias")
        act_step, dve_step, pool_step = sem("act_step"), sem("dve_step"), sem("pool_step")

        class Chain:

            def __init__(self, eng, s):
                self.eng, self.s, self.n = eng, s, 0

            def count(self, ins):
                self.n += 1
                ins.then_inc(self.s, 1)

            def wait(self):
                self.eng.wait_ge(self.s, self.n)

            def __call__(self, ins):
                self.count(ins)
                self.wait()

        class Banks:

            def __init__(self):
                self.n = {}

            def take(self, pe, name):
                u = self.n[name] = len(self.n)
                if u >= 2:
                    pe.wait_ge(bank_free[u % 2], u // 2)
                return side_ps[u % 2]

            def ps(self, name):
                return side_ps[self.n[name] % 2]

            def fill(self, ins, name):
                ins.then_inc(bank_full[self.n[name] % 2], 1)

            def wait(self, eng, name):
                u = self.n[name]
                eng.wait_ge(bank_full[u % 2], u // 2 + 1)

            def free(self, ins, name):
                ins.then_inc(bank_free[self.n[name] % 2], 1)

            def wait_free(self, eng, name):
                u = self.n[name]
                eng.wait_ge(bank_free[u % 2], u // 2 + 1)

        def split3(out, w, x_parts, first=True, last=True):
            nc.tensor.matmul(out, w[0], x_parts[0], start=first, stop=False)
            nc.tensor.matmul(out, w[0], x_parts[1], start=False, stop=False)
            return nc.tensor.matmul(out, w[1], x_parts[0], start=False, stop=last)

        def pairs(rows_d):
            return rows_d.rearrange("(i r) l d -> i r l d", r=2)

        def rows(x):
            return x[:, :, :].rearrange("p t d -> p (t d)")

        ident = pk("ident")
        xn_arena = arena[:, 0, :].rearrange("p (t d) -> p t d", t=TT)
        xn_out = ffn_out[:, :].rearrange("p (t d) -> p t d", t=TT)
        x_raw = arena[:, 3, :].rearrange("p (t d) -> p t d", t=TT)


        def norm_dve(dve, link, kind, k, x, xn):
            stats, rstd_done, out = ln_sems[kind]
            for t in range(TT):
                link.count(nc.vector.bn_stats(bn6[:, t, :], x[:, t, :]))
            link.wait()
            for t in range(TT):
                nc.vector.bn_aggr(mv[:, t, :], bn6[:, t, :]).then_inc(stats, 1)
            yield 1
            dve.wait_ge(rstd_done, k + 1)
            for t in range(TT):
                nc.vector.tensor_scalar(xn[:, t, :], x[:, t, :], mv[:, t, 0:1], rstd[:, t:t + 1],
                                        ALU.subtract, ALU.mult).then_inc(out, 1)

        def norm_pool(pool, link, kind, k):
            stats, rstd_done, _ = ln_sems[kind]
            pool.wait_ge(stats, TT * (k + 1))
            link(nc.gpsimd.tensor_scalar(rstd[:, :], mv[:, :, 1], EPS, None, ALU.add))
            nc.gpsimd.tensor_tensor(rstd[:, :], rstd[:, :], half[:, :], ALU.pow).then_inc(rstd_done, 1)

        def norm_pe(pe, b, kind, k, name, xn):
            ps = b.take(pe, name)
            pe.wait_ge(ln_sems[kind][2], TT * (k + 1))
            for t in range(TT):
                last = nc.tensor.transpose(ps[:, t * P:(t + 1) * P], xn[:, t, :], ident)
            b.fill(last, name)

        class Finish:
            @staticmethod
            def programs():
                return dict(pe=Finish.pe, dve=Finish.dve)

            @staticmethod
            def pe(pe, link, b, ph, k):
                yield ph.o
                name = (ph, "fin")
                ps = b.take(pe, name)
                if not ph.first:
                    pe.wait_ge(ffn_ready, ph.m)
                for t in range(TT):
                    last = nc.tensor.transpose(ps[:, t * P:(t + 1) * P], ffn_out[:, t * P:(t + 1) * P], ident)
                b.fill(last, name)

            @staticmethod
            def dve(dve, link, b, ph, k):
                yield ph.o
                name, (src, dst) = (ph, "fin"), ph.fin
                b.wait(dve, name)
                b.free(nc.vector.tensor_tensor(rows(dst), b.ps(name)[:, :], rows(src), ALU.add), name)
                b.wait_free(dve, name)

        class Head:
            @staticmethod
            def programs():
                return dict(pe=Head.pe, act=Head.act, dve=Head.dve, pool=Head.pool)

            @staticmethod
            def pe(pe, link, b, ph, k):
                t0, slot = ph.t_head, ph.slot
                yield t0 + 2
                norm_pe(pe, b, "ffn_ln", k, (ph, "ln2"), xn_arena)
                yield t0 + 4
                name = (ph, "route")
                ps = b.take(pe, name)
                pe.wait_ge(fx_f32, k + 1)
                for t in range(TT):
                    last = nc.tensor.matmul(ps[:, t * 2 * E:(t + 1) * 2 * E], fx[slot][:, t * P:(t + 1) * P],
                                            pk("w_route"), start=True, stop=True)
                b.fill(last, name)
                yield t0 + 7, 1
                name = (ph, "mixT")
                ps = b.take(pe, name)
                pe.wait_ge(mix_ready, k + 1)
                for t in range(TT):
                    last = nc.tensor.transpose(ps[0:2 * E, t * P:(t + 1) * P], cwhl[:, t, :], ident)
                b.fill(last, name)

            @staticmethod
            def act(act, link, b, ph, k):
                t0, slot = ph.t_head, ph.slot
                yield t0 + 3
                b.wait(act, (ph, "ln2"))
                ps = b.ps((ph, "ln2"))
                nc.scalar.copy(fx[slot][:, :], ps[:, :]).then_inc(fx_f32, 1)
                nc.scalar.copy(fxh[slot][:, :], ps[:, :]).then_inc(fx_hi, 1)
                yield t0 + 5
                b.wait_free(act, (ph, "route"))
                nc.scalar.activation(lg[:, :, 0, :], lg[:, :, 0, :], ACT.Exp).then_inc(route_exp, 1)
                nc.scalar.activation(lg[:, :, 1, :], lg[:, :, 1, :], ACT.Exp, scale=10.0).then_inc(route_exp, 1)
                yield t0 + 7, 1
                b.wait(act, (ph, "mixT"))
                b.free(nc.scalar.copy(cwT[slot], b.ps((ph, "mixT"))[0:2 * E, :]), (ph, "mixT"))

            @staticmethod
            def dve(dve, link, b, ph, k):
                t0, slot = ph.t_head, ph.slot
                yield t0
                for s in norm_dve(dve, link, "ffn_ln", k, ph.x_out, xn_arena):
                    yield t0 + s
                yield t0 + 4
                dve.wait_ge(fx_hi, k + 1)
                b.free(nc.vector.tensor_tensor(fxl[slot][:, :], b.ps((ph, "ln2"))[:, :],
                                               fxh[slot][:, :].bitcast(F32), ALU.subtract), (ph, "ln2"))
                yield t0 + 5
                name = (ph, "route")
                b.wait(dve, name)
                lps = b.ps(name)[:, 0:TT * 2 * E].rearrange("p (t k e) -> p t k e", t=TT, k=2)
                link(nc.vector.reduce_max(lmax[:, :, :], lps, AX))
                b.free(nc.vector.tensor_tensor(lg[:, :, :, :], lps,
                                               lmax[:, :, :].unsqueeze(3).broadcast_to([P, TT, 2, E]), ALU.subtract), name)
                yield t0 + 6
                dve.wait_ge(route_exp, 2 * (k + 1))
                link(nc.vector.reduce_sum(cws[:, :, :], lg[:, :, :, :], AX))
                link(nc.vector.reciprocal(cws[:, :, :], cws[:, :, :]))
                link(nc.vector.tensor_tensor(lg[:, :, :, :], lg[:, :, :, :],
                                             cws[:, :, :].unsqueeze(3).broadcast_to([P, TT, 2, E]), ALU.mult))
                link(nc.vector.tensor_tensor(cw[:, :, :], lg[:, :, 0, :], lg[:, :, 1, :], ALU.mult))
                link(nc.vector.reduce_sum(cws[:, :, 0], cw[:, :, :], AX))
                link(nc.vector.tensor_scalar(cws[:, :, 0], cws[:, :, 0], 1e-9, None, ALU.add))
                link(nc.vector.reciprocal(cws[:, :, 1], cws[:, :, 0]))
                link(nc.vector.tensor_tensor(cw[:, :, :], cw[:, :, :],
                                             cws[:, :, 1].unsqueeze(2).broadcast_to([P, TT, E]), ALU.mult))
                link(nc.vector.tensor_copy(cwh[:, :, :], cw[:, :, :]))
                link.count(nc.vector.tensor_copy(cwhl[:, :, 0:E], cwh[:, :, :].bitcast(F32)))
                nc.vector.tensor_tensor(cwhl[:, :, E:2 * E], cw[:, :, :], cwh[:, :, :].bitcast(F32),
                                        ALU.subtract).then_inc(mix_ready, 1)

            @staticmethod
            def pool(pool, link, b, ph, k):
                yield ph.t_head
                norm_pool(pool, link, "ffn_ln", k)

        class Ssm:
            @staticmethod
            def programs():
                return dict(pe=Ssm.pe, act=Ssm.act, dve=Ssm.dve, pool=Ssm.pool)

            @staticmethod
            def pe(pe, link, b, ph, k0):
                yield 2
                norm_pe(pe, b, "ssm_ln", k0, (ph, "ln1"), xn_arena)
                yield 4
                ps = b.take(pe, (ph, "win"))
                b.wait_free(pe, (ph, "ln1"))
                b.fill(nc.tensor.matmul(ps[:, :], pk("w_in"), sxT, start=True, stop=True), (ph, "win"))
                yield 8
                pe.wait_ge(xs_done, k0 + 1)
                ps = b.take(pe, (ph, "dt"))
                for v in range(2):
                    last = nc.tensor.matmul(ps[:, :], wdt[v][:, :], xs, start=v == 0, stop=v == 1)
                b.fill(last, (ph, "dt"))
                for k in range(KT):
                    for w, name in ((0, (ph, "b", k)), (DSTATE, (ph, "c", k))):
                        yield 9 + 3 * k + (1.5 if w else 0)
                        ps = b.take(pe, name)
                        for v in range(2):
                            last = nc.tensor.matmul(ps[:, :],
                                                    wbc[v][:, w + 2 * k:w + 2 * k + 2, :].rearrange("p a b -> p (a b)"),
                                                    xs, start=v == 0, stop=v == 1)
                        b.fill(last, name)
                yield 24
                ps = b.take(pe, (ph, "proj"))
                pe.wait_ge(y_done, KT * (k0 + 1))
                for t in range(TT):
                    out = ps[:, t * P:(t + 1) * P]
                    nc.tensor.matmul(out, tot[:, t * P:(t + 1) * P], pk("w_out_y"), start=True, stop=False)
                    last = nc.tensor.matmul(out, zb[0:INNER, t * P:(t + 1) * P], pk("w_out_z")[0:INNER, :],
                                            start=False, stop=True)
                b.fill(last, (ph, "proj"))

            @staticmethod
            def act(act, link, b, ph, k0):
                yield 3
                b.wait(act, (ph, "ln1"))
                b.free(nc.scalar.copy(sxT, b.ps((ph, "ln1"))[:, :]), (ph, "ln1"))
                yield 6
                b.wait_free(act, (ph, "win"))
                nc.scalar.activation(xb2[0:INNER, :], cv[0:INNER, :], ACT.Silu).then_inc(silu_x, 1)
                nc.scalar.activation(xb2[INNER:P, :], cv[0:INNER, :], ACT.Silu).then_inc(silu_x, 1)
                nc.scalar.activation(zb[0:INNER, :], cv[INNER:P, :], ACT.Silu).then_inc(silu_x, 1)
                act.wait_ge(silu_x, 3 * k0 + 2)
                nc.scalar.activation(xsm, xb2, ACT.Copy, scale=pk("lo_ssm")).then_inc(xs_m, 1)
                yield 9
                b.wait_free(act, (ph, "dt"))
                link(nc.scalar.activation(delta, delta, ACT.Exp))
                yield 10
                nc.scalar.activation(delta, delta, ACT.Ln, bias=1.0).then_inc(dt_soft, 1)
                for k in range(KT):
                    yield 10 + 3 * k
                    if k >= 1:
                        act.wait_ge(scan_done, KT * k0 + k)
                    b.wait(act, (ph, "b", k))
                    b.free(nc.scalar.activation(btile, b.ps((ph, "b", k))[:, :], ACT.Tanh), (ph, "b", k))
                    yield 11 + 3 * k
                    if k >= 2:
                        act.wait_ge(y_done, KT * k0 + k - 1)
                    b.wait(act, (ph, "c", k))
                    b.free(nc.scalar.activation(ctile[:, k % 2, :], b.ps((ph, "c", k))[:, :], ACT.Tanh, scale=-1.0),
                           (ph, "c", k))
                    if k == 0:
                        yield 11.5
                        act.wait_ge(delta_done, k0 + 1)
                    if k in (0, 2):
                        yield 11 + 3 * k
                        for kk in (k, k + 1):
                            if kk >= 2:
                                act.wait_ge(y_part, KT * k0 + kk - 1)
                            nc.scalar.activation(dec[:, kk % 2, :], delta, ACT.Exp,
                                                 scale=neg_a[:, kk:kk + 1]).then_inc(dec_exp, 1)

            @staticmethod
            def dve(dve, link, b, ph, k0):
                yield 0.5
                dve.wait_ge(raw_loaded, 16 * (k0 + 1))
                for s in norm_dve(dve, link, "ssm_ln", k0, x_raw, xn_arena):
                    yield s
                yield 5
                b.wait(dve, (ph, "win"))
                ps, kc = b.ps((ph, "win")), pk("k_conv")
                link(nc.vector.tensor_scalar(cv, ps[:, :], kc[:, 1:2], None, ALU.mult))
                link(nc.vector.scalar_tensor_tensor(cv[:, 1:L], ps[:, 0:L - 1], kc[:, 0:1], cv[:, 1:L], ALU.mult, ALU.add))
                b.free(nc.vector.scalar_tensor_tensor(cv[:, 0:L - 1], ps[:, 1:L], kc[:, 2:3], cv[:, 0:L - 1],
                                                      ALU.mult, ALU.add), (ph, "win"))
                yield 7
                dve.wait_ge(xs_m, k0 + 1)
                nc.vector.tensor_tensor(xs, xb2, xsm.bitcast(F32), ALU.subtract).then_inc(xs_done, 1)
                yield 8.5
                b.wait(dve, (ph, "dt"))
                b.free(nc.vector.tensor_scalar(delta, b.ps((ph, "dt"))[:, :], pk("b_dt"), 20.0, ALU.add, ALU.min),
                       (ph, "dt"))
                yield 11
                dve.wait_ge(dt_soft, k0 + 1)
                nc.vector.tensor_scalar(delta, delta, 1e-4, 1.0, ALU.max, ALU.min).then_inc(delta_done, 1)
                for k in range(KT):
                    yield 12 + 3 * k
                    d = dec[:, k % 2, :]
                    dve.wait_ge(dec_exp, KT * k0 + k + 1)
                    link(nc.vector.tensor_scalar(d, d, 1e-4, 1.0, ALU.max, ALU.min))
                    dve.wait_ge(bx_done, KT * k0 + k + 1)
                    link(nc.vector.scalar_tensor_tensor(btile, d, 1.0, btile, ALU.subtract, ALU.mult))
                    nc.vector.tensor_tensor_scan(d, d, btile, 0.0, ALU.mult, ALU.add).then_inc(scan_done, 1)
                    yield 14 + 3 * k
                    dve.wait_ge(y_part, KT * k0 + k + 1)
                    if k == 0:
                        ins = nc.vector.scalar_tensor_tensor(tot, xb2, pk("d_skip"), ctile[:, 0, :], ALU.mult, ALU.add)
                    else:
                        dve.wait_ge(y_done, KT * k0 + k)
                        ins = nc.vector.tensor_tensor(tot, tot, ctile[:, k % 2, :], ALU.add)
                    ins.then_inc(y_done, 1)
                yield 24
                b.wait(dve, (ph, "proj"))
                dve.wait_ge(res_loaded, 16 * (k0 + 1))
                b.free(nc.vector.tensor_tensor(rows(ph.x_out), b.ps((ph, "proj"))[:, :], rows(ph.x_out), ALU.add),
                       (ph, "proj"))
                b.wait_free(dve, (ph, "proj"))

            @staticmethod
            def pool(pool, link, b, ph, k0):
                yield 0.5
                norm_pool(pool, link, "ssm_ln", k0)
                for k in range(KT):
                    yield 11 + 3 * k
                    b.wait_free(pool, (ph, "b", k))
                    nc.gpsimd.tensor_tensor(btile, btile, xb2, ALU.mult).then_inc(bx_done, 1)
                    yield 13 + 3 * k
                    b.wait_free(pool, (ph, "c", k))
                    pool.wait_ge(scan_done, KT * k0 + k + 1)
                    c = ctile[:, k % 2, :]
                    nc.gpsimd.tensor_tensor(c, c, dec[:, k % 2, :], ALU.mult).then_inc(y_part, 1)

        class Pre:
            @staticmethod
            def programs():
                return dict(pe=Pre.pe, act=Pre.act, dve=Pre.dve, pool=Pre.pool)

            @staticmethod
            def pe(pe, link, b, ph, k):
                t0 = ph.t_pre
                yield t0 + 4
                norm_pe(pe, b, "att_ln", k, (ph, "ln3"), xn_out)
                for g in range(4):
                    yield t0 + 6 + g
                    if g == 0:
                        b.wait_free(pe, (ph, "ln3"))
                    for w, name in ((wq, (ph, "q", g)), (wk, (ph, "k", g))):
                        ps = b.take(pe, name)
                        wa = [w[v][:, g, :, :, :].rearrange("p a b c -> p (a b c)") for v in range(2)]
                        b.fill(split3(ps[:, :], wa, (axh[:, 0:L], axl[:, 0:L])), name)

            @staticmethod
            def act(act, link, b, ph, k):
                t0 = ph.t_pre
                yield t0 + 4
                b.wait(act, (ph, "ln3"))
                nc.scalar.copy(axh[:, 0:L], b.ps((ph, "ln3"))[:, :]).then_inc(x_hi, 1)
                for g in range(4):
                    yield t0 + 6 + g
                    for j, v in enumerate("qk"):
                        b.wait(act, (ph, v, g))
                        dst = q3[:, g, :] if v == "q" else k3[:, g, 0:L]
                        nc.scalar.activation(dst, b.ps((ph, v, g))[:, :], ACT.Identity,
                                             bias=bq_lo[:, 4 * j + g:4 * j + g + 1], scale=pk("lo_" + v)).then_inc(q_lo_m, 1)

            @staticmethod
            def dve(dve, link, b, ph, k):
                t0 = ph.t_pre
                yield t0
                for s in norm_dve(dve, link, "att_ln", k, x2, xn_out):
                    yield t0 + 2 * s
                yield t0 + 5
                dve.wait_ge(x_hi, k + 1)
                b.free(nc.vector.tensor_tensor(axl[:, 0:L], b.ps((ph, "ln3"))[:, :], axh[:, 0:L].bitcast(F32),
                                               ALU.subtract), (ph, "ln3"))
                for g in range(4):
                    yield t0 + 6 + g
                    for j, v in enumerate("qk"):
                        dve.wait_ge(q_lo_m, 8 * k + 2 * g + j + 1)
                        dst = q3[:, g, :] if v == "q" else k3[:, g, 0:L]
                        b.free(nc.vector.scalar_tensor_tensor(dst, b.ps((ph, v, g))[:, :], pk("b_" + v)[:, g:g + 1],
                                                              dst.bitcast(F32), ALU.add, ALU.subtract), (ph, v, g))

            @staticmethod
            def pool(pool, link, b, ph, k):
                yield ph.t_pre
                norm_pool(pool, link, "att_ln", k)

        UNITS = [(i, p) for i in range(NQT) for p in range(2)]
        NUNIT = len(UNITS)

        def size(i):
            nq = min(QT, L - i * QT)
            left = LEFT if i else 0
            return nq, nq + left, i * QT - left, LEFT - left

        class Att:
            @staticmethod
            def programs():
                return dict(pe=Att.pe, act=Att.act, dve=Att.dve, pool=Att.pool)

            @staticmethod
            def at(ph, n):
                return ph.t_att + 0.5 + n * ph.pace

            @staticmethod
            def end(ph):
                return Att.at(ph, NUNIT + 1)

            @staticmethod
            def pe(pe, link, b, ph, k):
                at = lambda n: Att.at(ph, n)
                for half_v in range(2):
                    yield ph.t_att
                    name = (ph, "v", half_v)
                    ps = b.take(pe, name)
                    for i in range(4 * half_v, min(NQT, 4 * half_v + 4)):
                        _, nk, k0, _ = size(i)
                        nke = nk + nk % 2
                        out = ps[0:nke, (i % 4) * P:(i % 4 + 1) * P]
                        xw = [a[:, k0:k0 + nke] for a in (axh, axl)]
                        nc.tensor.matmul(out, xw[0], wv[0][:, :], start=True, stop=False)
                        nc.tensor.matmul(out, xw[1], wv[0][:, :], start=False, stop=False)
                        last = nc.tensor.matmul(out, xw[0], wv[1][:, :], start=False, stop=True)
                    b.fill(last, name)

                def scores(n):
                    i, p = UNITS[n]
                    nq, nk, k0, _ = size(i)
                    nke = nk + nk % 2
                    for rr in range(2):
                        r, name = 2 * p + rr, (ph, "s", n, rr)
                        ps = b.take(pe, name)
                        for g in range(4):
                            last = nc.tensor.matmul(ps[0:nq, g * KW:g * KW + nke],
                                                    q3[32 * r:32 * r + 32, g, i * QT:i * QT + nq],
                                                    k3[32 * r:32 * r + 32, g, k0:k0 + nke], start=True, stop=True)
                        b.fill(last, name)

                yield at(0)
                if ph.m > 0 or ph.pre:
                    b.wait_free(pe, ph.pre_ends[0])
                    b.wait_free(pe, ph.pre_ends[1])
                scores(0)
                for n in range(NUNIT):
                    i, p = UNITS[n]
                    nq, nk, _, _ = size(i)
                    if n + 1 < NUNIT:
                        yield at(n + 1)
                        scores(n + 1)
                    yield at(n + 2) - 0.5
                    pe.wait_ge(s_exp, NUNIT * k + n + 1)
                    for rr in range(2):
                        name = (ph, "t", n, rr)
                        ps = b.take(pe, name)
                        for g in range(4):
                            last = nc.tensor.transpose(ps[0:nk, g * QT:g * QT + nq], s_u[n % 2][0:nq, rr, g, 0:nk],
                                                       ident[0:nq, 0:nq])
                        b.fill(last, name)
                    yield at(n + 2)
                    name = (ph, "o", n)
                    ps = b.take(pe, name)
                    b.wait_free(pe, (ph, "t", n, 0))
                    b.wait_free(pe, (ph, "t", n, 1))
                    if n == 0:
                        b.wait_free(pe, (ph, "v", 1))
                    for rr in range(2):
                        for g in range(4):
                            h = 4 * g + 2 * p + rr
                            last = nc.tensor.matmul(ps[0:nq, (rr * 4 + g) * 9:(rr * 4 + g + 1) * 9],
                                                    pt_u[0:nk, rr, g, 0:nq], v_t[0:nk, i, h, :], start=True, stop=True)
                    b.fill(last, name)
                yield Att.end(ph) + 1
                ps = b.take(pe, (ph, "attT"))
                b.wait_free(pe, (ph, "o", NUNIT - 1))
                for i in range(NQT):
                    nq = size(i)[0]
                    last = nc.tensor.transpose(ps[:, i * QT:i * QT + nq], att[0:nq, i, :], ident[0:nq, 0:nq])
                b.fill(last, (ph, "attT"))
                yield Att.end(ph) + 2
                ps = b.take(pe, (ph, "proj"))
                b.wait_free(pe, (ph, "attT"))
                for t in range(TT):
                    last = nc.tensor.matmul(ps[:, t * P:(t + 1) * P], attT[:, t * P:(t + 1) * P], pk("w_o"),
                                            start=True, stop=True)
                b.fill(last, (ph, "proj"))

            @staticmethod
            def act(act, link, b, ph, k):
                at = lambda n: Att.at(ph, n)
                for n in range(NUNIT):
                    i, p = UNITS[n]
                    nq, nk, _, _ = size(i)
                    yield at(n + 1)
                    act.wait_ge(s_sub, NUNIT * k + n + 1)
                    u = s_u[n % 2][0:nq, :, :, 0:nk]
                    nc.scalar.activation(u, u, ACT.Exp, scale=float(HD) ** -0.5).then_inc(s_exp, 1)
                    yield at(n + 2) - 0.5
                    if n >= 1:
                        b.wait(act, (ph, "o", n - 1))
                    for rr in range(2):
                        name = (ph, "t", n, rr)
                        b.wait(act, name)
                        ps = b.ps(name)[0:nk, 0:4 * QT].rearrange("p (g q) -> p g q", g=4)[:, :, 0:nq]
                        b.free(nc.scalar.copy(pt_u[0:nk, rr, :, 0:nq], ps), name)
                yield Att.end(ph) + 1
                b.wait(act, (ph, "attT"))
                b.free(nc.scalar.copy(attT, b.ps((ph, "attT"))[:, :]), (ph, "attT"))

            @staticmethod
            def dve(dve, link, b, ph, k):
                at = lambda n: Att.at(ph, n)
                yield ph.t_att
                link(nc.vector.memset(v_t[:, :, :, HD:HD + 1], 1.0))
                for half_v in range(2):
                    b.wait(dve, (ph, "v", half_v))
                    lo, hi = 4 * half_v, min(NQT, 4 * half_v + 4)
                    for i in range(lo, hi):
                        nk = size(i)[1]
                        ins = nc.vector.tensor_tensor(
                            v_t[0:nk, i, :, 0:HD],
                            b.ps((ph, "v", half_v))[0:nk, (i % 4) * P:(i % 4 + 1) * P].rearrange("p (h e) -> p h e", e=HD),
                            pk("b_v")[0:nk, :].rearrange("p (h e) -> p h e", e=HD), ALU.add)
                        if i == hi - 1:
                            b.free(ins, (ph, "v", half_v))
                        else:
                            link.count(ins)

                def masked(n):
                    i, p = UNITS[n]
                    nq, nk, _, m0 = size(i)
                    mask = pk("mask")[:, m0:m0 + nk]
                    if n >= 2:
                        b.wait(dve, (ph, "t", n - 2, 1))
                    for rr in range(2):
                        name = (ph, "s", n, rr)
                        b.wait(dve, name)
                        ps = b.ps(name)[0:nq, 0:4 * KW].rearrange("p (g k) -> p g k", g=4)[:, :, 0:nk]
                        b.free(nc.vector.tensor_tensor(s_u[n % 2][0:nq, rr, :, 0:nk], ps,
                                                       mask[0:nq, :].unsqueeze(1).broadcast_to([nq, 4, nk]), ALU.add),
                               name)
                    b.wait_free(dve, (ph, "s", n, 0))
                    b.wait_free(dve, (ph, "s", n, 1))
                    if n >= 1:
                        dve.wait_ge(s_sub, NUNIT * k + n)
                    nc.vector.reduce_max(smax[0:nq, :, :], s_u[n % 2][0:nq, :, :, 0:nk], AX).then_inc(s_max, 1)

                def normalised(n):
                    i, p = UNITS[n]
                    nq = size(i)[0]
                    name = (ph, "o", n)
                    b.wait(dve, name)
                    ps = b.ps(name)[0:nq, 0:72].rearrange("p (r g e) -> p r g e", r=2, g=4)
                    link(nc.vector.reciprocal(rinv[0:nq, :, :], ps[:, :, :, HD]))
                    b.free(nc.vector.tensor_tensor(
                        att[0:nq, i, :].rearrange("p (g r e) -> p r g e", g=4, r=4)[:, 2 * p:2 * p + 2, :, :],
                        ps[:, :, :, 0:HD], rinv[0:nq, :, :].unsqueeze(3).broadcast_to([nq, 2, 4, HD]), ALU.mult), name)

                for n in range(NUNIT + 2):
                    yield at(n)
                    if n >= 2:
                        normalised(n - 2)
                    if n < NUNIT:
                        masked(n)
                yield Att.end(ph) + 2
                b.wait(dve, (ph, "proj"))
                dve.wait_ge(x2_bias, k + 1)
                if ph.store is not None:
                    dve.wait_ge(stored, 16 * ph.store_n)
                b.free(nc.vector.tensor_tensor(rows(ph.x_out), b.ps((ph, "proj"))[:, :], rows(x2), ALU.add), (ph, "proj"))
                b.wait_free(dve, (ph, "proj"))

            @staticmethod
            def pool(pool, link, b, ph, k):
                yield ph.t_att
                if ph.pre:
                    pool.wait_ge(ln_sems["att_ln"][2], TT * ph.pre_n)
                nc.gpsimd.tensor_tensor(x2[:, :, :], x2[:, :, :], pk("b_o").unsqueeze(1).broadcast_to([P, TT, D]),
                                        ALU.add).then_inc(x2_bias, 1)
                for n in range(NUNIT):
                    i, p = UNITS[n]
                    nq, nk, _, _ = size(i)
                    yield Att.at(ph, n) + 0.5
                    pool.wait_ge(s_max, NUNIT * k + n + 1)
                    for rr in range(2):
                        u = s_u[n % 2][0:nq, rr, :, 0:nk]
                        ins = nc.gpsimd.tensor_tensor(u, u, smax[0:nq, rr, :].unsqueeze(2).broadcast_to([nq, 4, nk]),
                                                      ALU.subtract)
                        if rr == 0:
                            link(ins)
                        else:
                            ins.then_inc(s_sub, 1)


        class Phase:

            def __init__(self, main=None, fin=None, ssm=False, pre=False, att=False, slot=0, x_out=None,
                         load=None, store=None, form="silu", hh_act=(), pace=2, t_pre=0, t_att=0, t_head=0):
                self.main, self.fin, self.ssm, self.pre, self.att = main, fin, ssm, pre, att
                self.slot, self.x_out, self.load, self.store = slot, x_out, load, store
                self.form, self.hh_act, self.pace = form, hh_act, pace
                self.t_pre, self.t_att, self.t_head = t_pre, t_att, t_head
                if att:
                    self.t_head = Att.end(self) + 2

            def stages(self):
                out = []
                for on, cls, k in ((self.fin, Finish, 0), (self.ssm, Ssm, self.ssm_n), (self.pre, Pre, self.pre_n - 1),
                                   (self.att, Att, self.att_n), (self.x_out is not None, Head, self.head_n)):
                    if on:
                        out.append((cls, k))
                return out

        def run_block(phases, setup=False):
            b = Banks()
            counts = dict(ssm=0, pre=0, att=0, head=0, store=0)
            for m, ph in enumerate(phases):
                ph.m, ph.first, ph.o = m, m == 0, 0 if m == 0 else 5
                ph.ssm_n, ph.att_n, ph.head_n = counts["ssm"], counts["att"], counts["head"]
                counts["ssm"] += ph.ssm
                counts["pre"] += ph.pre
                counts["att"] += ph.att
                counts["head"] += ph.x_out is not None
                counts["store"] += ph.store is not None
                ph.pre_n, ph.store_n = counts["pre"], counts["store"]
                owner = ph if ph.pre else phases[m - 1]
                ph.pre_ends = ((owner, "q", 3), (owner, "k", 3))
            mains = [ph for ph in phases if ph.main is not None]
            assert mains == phases[:len(mains)]
            NC = NCH * len(mains)
            steps_n = NC + LAG + 1 if mains else 0
            ring, at_ring = {}, 0
            for c in range(NC + 1):
                for use in ([("g", c)] if c < NC else []) + ([("mix", c // CPE)] if c % CPE == 0 and c < NC and c % NCH == 0
                                                             else [("mix", c // CPE + 1)] if c % CPE == 2 and (c + 2) % NCH and c < NC else []):
                    ring[use] = at_ring
                    at_ring += 1
            uses = {v: k for k, v in ring.items()}

            def of(c):
                return phases[c // NCH]

            def hh_eng(c):
                return "act" if c % 4 in of(c).hh_act else "dve"

            def hh_count(c):
                return sum(hh_eng(x) == hh_eng(c) for x in range(c + 1))

            def reads(c):
                n = sum(of(x).form == of(c).form for x in range(c + 1))
                return (gate_done, c + 1) if of(c).form == "silu" else (gated, n)

            def w_part(j, v):
                return (wg, wu, wd)[j // E][v][:, CPE * (j % E):CPE * (j % E + 1), :].rearrange("p a b -> p (a b)")

            def interleave(engine, eng, link, steps):
                streams = []

                def place(ph, slot):
                    slot, late = slot if isinstance(slot, tuple) else (slot, 0)
                    return NCH * ph.m + (min(slot, NCH - 1 + late) if ph.m < len(phases) - 1 else slot)

                for ph in phases:
                    for cls, k in ph.stages():
                        if engine in cls.programs():
                            gen = cls.programs()[engine](eng, link, b, ph, k)
                            streams.append([place(ph, next(gen)), ph, gen])

                def run(c):
                    while streams:
                        first = min(streams, key=lambda s: s[0])
                        if first[0] > c:
                            return
                        slot = next(first[2], None)
                        if slot is None:
                            streams.remove(first)
                        else:
                            first[0] = max(first[0], place(first[1], slot))

                for c, step in enumerate(steps):
                    rest = step()
                    for _ in rest or ():
                        run(c)
                    run(c + 0.5)
                run(10 ** 6)

            with nc.Block() as block:

                @block.tensor
                def _(pe):
                    def gate_bank(use):
                        n = ring[use]
                        if n >= 3:
                            kind, x = uses[n - 3]
                            if kind == "g":
                                pe.wait_ge(*reads(x))
                            else:
                                pe.wait_ge(xe_done, x + 1)
                        return pg[n % 3]

                    def mix(e):
                        main = of(CPE * e).main
                        ps = gate_bank(("mix", e))
                        if e % E == 0 and e > 0:
                            b.wait_free(pe, (phases[e // E - 1], "mixT"))
                        nc.tensor.matmul(ps[:, :], sel[32 * main:32 * main + 2 * E, e % E:e % E + 1].broadcast_to([2 * E, P]),
                                         cwT[main], start=True, stop=True).then_inc(mix_full, 1)

                    def chunk(c):
                        if c < NC:
                            main = of(c).main
                            if c % NCH == 0 and c:
                                b.wait_free(pe, (phases[c // NCH - 1], "ln2"))
                            ps = gate_bank(("g", c))
                            split3(ps[:, :], [w[:, c % NCH, :] for w in wg], (fxh[main][:, :], fxl[main][:, :])).then_inc(g_full, 1)
                            if c % CPE == 2 and (c + 2) % NCH:
                                mix(c // CPE + 1)
                        d = c - 1
                        if 0 <= d < NC:
                            e = d // CPE
                            if d >= 2:
                                pe.wait_ge(h_done, d - 1)
                            if d % CPE == 0:
                                pe.wait_ge(xel_done, e + 1)
                            split3(pu[d % 2][:, :], [w[:, d % NCH, :] for w in wu],
                                   (xeh[:, e % 2, :], xel[:, e % 2, :])).then_inc(u_full, 1)
                        yield
                        if c < NC and c % NCH == 0:
                            mix(c // CPE)
                        d = c - LAG
                        if 0 <= d < NC:
                            if d % NCH == 0 and d:
                                pe.wait_ge(ffn_ready, d // NCH)
                            pe.wait_ge(hl_done, d + 1)
                            split3(pd[:, :], [w[:, d % NCH, :] for w in wd], (hh_b[:, d % 3, :], hl_b[:, d % 3, :]),
                                   first=d % NCH == 0, last=d % NCH == NCH - 1).then_inc(down_done, 1)

                    if setup:
                        pe.wait_ge(packed, 32)
                        nc.tensor.matmul(pg[0][:, 0:P], pk("w_dtx")[0:DTRANK, :], pk("w_dt")[0:DTRANK, :],
                                         start=True, stop=True).then_inc(wdt_full, 1)
                        pe.wait_ge(w_small, 1)
                    interleave("pe", pe, None, [lambda c=c: chunk(c) for c in range(steps_n)])

                @block.sync
                def _(sp):
                    if setup:
                        sp.dma_start(raw, pack_d[:, 0:NRAW]).then_inc(packed, 16)
                        sp.dma_start(pack[:, :], pack_d[:, NRAW:NPACK]).then_inc(packed, 16)
                    for m, ph in enumerate(phases):
                        if ph.load is not None:
                            src = pairs(x_d)[ph.load[0]][ph.load[1]].rearrange("(t p) d -> p t d", p=P)
                            if m:
                                b.wait(sp, (phases[m - 1], "proj"))
                            sp.dma_start(x_raw, src).then_inc(raw_loaded, 16)
                            if ph.fin:
                                b.wait_free(sp, (ph, "fin"))
                            sp.dma_start(ph.x_out[:, :, :], src).then_inc(res_loaded, 16)
                        if setup:
                            for j in range(3 * E):
                                if j >= 3:
                                    sp.wait_ge(w_lo, j - 2)
                                dst, src = h_b[:, j % 3, :], (wg_d, wu_d, wd_d)[j // E][j % E]
                                if j >= 2 * E:
                                    src = src.rearrange("(c p) h -> p c h", p=P)
                                    dst = dst.rearrange("p (c h) -> p c h", h=P)
                                sp.dma_start(dst, src).then_inc(w_loaded[j % 3], 16)
                        if ph.store is not None:
                            b.wait_free(sp, (ph, "fin"))
                            sp.dma_start(pairs(out_d)[ph.store[0]][ph.store[1]].rearrange("(t p) d -> p t d", p=P), ph.fin[1][:, :, :]).then_inc(stored, 16)
                    if counts["store"]:
                        sp.wait_ge(stored, 16 * counts["store"])

                @block.scalar
                def _(act):
                    link = Chain(act, act_step)

                    def expert_hi(e):
                        act.wait_ge(xe_done, e + 1)
                        if e >= 2:
                            act.wait_ge(u_full, CPE * (e - 1))
                        nc.scalar.copy(xeh[:, e % 2, :], xe[:, :]).then_inc(xeh_done, 1)

                    def chunk(c):
                        if (c - LAG) % NCH == 0 and c >= NCH:
                            out_of(c // NCH - 1)
                        if c < NC:
                            act.wait_ge(g_full, c + 1)
                            if c >= 3:
                                act.wait_ge(hl_done, c - 2)
                            ps = pg[ring[("g", c)] % 3]
                            if of(c).form == "silu":
                                nc.scalar.activation(h_b[:, c % 3, :], ps[:, :], ACT.Silu).then_inc(gate_done, 1)
                            else:
                                nc.scalar.activation(h_b[:, c % 3, :], ps[:, :], ACT.Tanh, scale=0.5).then_inc(gate_done, 1)
                            if c % CPE == 3 and (c + 1) % NCH:
                                expert_hi(c // CPE + 1)
                        d = c - 2
                        if 0 <= d < NC and hh_eng(d) == "act":
                            act.wait_ge(h_done, d + 1)
                            if d >= 3:
                                act.wait_ge(down_done, d - 2)
                            nc.scalar.copy(hh_b[:, d % 3, :], h_b[:, d % 3, :]).then_inc(hh_done["act"], 1)
                        yield
                        if c < NC and c % NCH == 0:
                            expert_hi(c // CPE)

                    def out_of(m):
                        act.wait_ge(down_done, NCH * (m + 1))
                        if phases[m].fin:
                            b.wait(act, (phases[m], "fin"))
                        scale = 1.0 if phases[m].form == "silu" else 0.5
                        nc.scalar.mul(ffn_out[:, :], pd[:, :], scale).then_inc(ffn_ready, 1)

                    def split_w(j):
                        act.wait_ge(w_loaded[j % 3], 16 * (j // 3 + 1))
                        nc.scalar.copy(w_part(j, 0), h_b[:, j % 3, :]).then_inc(w_hi, 1)

                    if setup:
                        act.wait_ge(w_prep, 1)
                        link(nc.scalar.activation(neg_a[:, :], neg_a[:, :], ACT.Exp, scale=-1.0))
                        nc.scalar.activation(neg_a[:, :], neg_a[:, :], ACT.Ln, bias=1.0).then_inc(w_prep, 1)
                    steps = [lambda j=j: split_w(j) for j in range(3 * E)] if setup else [lambda c=c: chunk(c) for c in range(steps_n)]
                    interleave("act", act, link, steps)

                @block.vector
                def _(dve):
                    link = Chain(dve, dve_step)

                    def expert_in(e):
                        dve.wait_ge(mix_full, e + 1)
                        if e >= 1:
                            dve.wait_ge(xel_done, e)
                        nc.vector.tensor_tensor(xe[:, :], pg[ring[("mix", e)] % 3][:, :], fx[of(CPE * e).main][:, :],
                                                ALU.mult).then_inc(xe_done, 1)

                    def chunk(c):
                        d = c - 1
                        if 0 <= d < NC and of(d).form == "tanh":
                            h = h_b[:, d % 3, :]
                            dve.wait_ge(gate_done, d + 1)
                            nc.vector.scalar_tensor_tensor(h, h, 1.0, pg[ring[("g", d)] % 3][:, :], ALU.add,
                                                           ALU.mult).then_inc(gated, 1)
                        if 0 <= d < NC:
                            h = h_b[:, d % 3, :]
                            dve.wait_ge(*reads(d))
                            dve.wait_ge(u_full, d + 1)
                            nc.vector.tensor_tensor(h, pu[d % 2][:, :], h, ALU.mult).then_inc(h_done, 1)
                        if c < NC and c % CPE == 2 and (c + 2) % NCH:
                            expert_in(c // CPE + 1)
                        d = c - 2
                        if 0 <= d < NC and hh_eng(d) == "dve":
                            dve.wait_ge(h_done, d + 1)
                            if d >= 3:
                                dve.wait_ge(down_done, d - 2)
                            nc.vector.tensor_copy(hh_b[:, d % 3, :], h_b[:, d % 3, :]).then_inc(hh_done["dve"], 1)
                        yield
                        if c < NC and c % NCH == 0:
                            expert_in(c // CPE)

                    def split_w(j):
                        dve.wait_ge(w_hi, j + 1)
                        nc.vector.tensor_tensor(w_part(j, 1), h_b[:, j % 3, :], w_part(j, 0).bitcast(F32),
                                                ALU.subtract).then_inc(w_lo, 1)

                    def small_weights():
                        def both(dst, src):
                            link(nc.vector.tensor_copy(dst[0], src))
                            link(nc.vector.tensor_tensor(dst[1], src, dst[0].bitcast(F32), ALU.subtract))

                        dve.wait_ge(packed, 32)
                        link(nc.vector.tensor_scalar(mv[:, 0:TT, 0], pk("a_log"), -1.0, None, ALU.mult))
                        nc.vector.tensor_tensor(neg_a[:, :], mv[:, 0:TT, 0], pk("a_log"), ALU.max).then_inc(w_prep, 1)
                        for w, name in ((wq, "w_q"), (wk, "w_k")):
                            src = pk(name).rearrange("p (g h e) -> p g h e", g=4, h=4)
                            for g in range(4):
                                both([v[:, g, :, :, :] for v in w],
                                     src[:, g, :, :].unsqueeze(2).broadcast_to([P, 4, 4, HD]))
                        both([w[:, :] for w in wv], pk("w_v"))
                        both([w[:, :, :] for w in wbc], pk("w_bc").unsqueeze(2).broadcast_to([P, 2 * DSTATE, INNER]))
                        link(nc.vector.tensor_copy(sel[:, :], pk("sel")[0:32 + 2 * E, :]))
                        dve.wait_ge(wdt_full, 1)
                        link(nc.vector.tensor_copy(xe[:, 0:P], pg[0][:, 0:P]))
                        both([w[:, :] for w in wdt], xe[:, 0:P])
                        for j, v in enumerate("qk"):
                            link(nc.vector.tensor_scalar(bq_lo[:, 4 * j:4 * j + 4], pk("b_" + v), pk("lo_" + v), None, ALU.mult))
                        dve.wait_ge(w_prep, 2)
                        link(nc.vector.scalar_tensor_tensor(neg_a[:, :], pk("a_log"), 0.0, neg_a[:, :], ALU.max, ALU.add))
                        nc.vector.tensor_scalar(neg_a[:, :], neg_a[:, :], -1.0, -1e-4, ALU.mult, ALU.add).then_inc(w_small, 1)
                        dve.wait_ge(w_small, 1)

                    if setup:
                        small_weights()
                    steps = [lambda j=j: split_w(j) for j in range(3 * E)] if setup else [lambda c=c: chunk(c) for c in range(steps_n)]
                    interleave("dve", dve, link, steps)

                @block.gpsimd
                def _(pool):
                    link = Chain(pool, pool_step)

                    def expert_lo(e):
                        pool.wait_ge(xeh_done, e + 1)
                        nc.gpsimd.tensor_tensor(xel[:, e % 2, :], xe[:, :], xeh[:, e % 2, :].bitcast(F32),
                                                ALU.subtract).then_inc(xel_done, 1)

                    def chunk(c):
                        if c < NC and c % CPE == 3 and (c + 1) % NCH:
                            expert_lo(c // CPE + 1)
                        d = c - 2
                        if 0 <= d < NC:
                            pool.wait_ge(hh_done[hh_eng(d)], hh_count(d))
                            nc.gpsimd.tensor_tensor(hl_b[:, d % 3, :], h_b[:, d % 3, :], hh_b[:, d % 3, :].bitcast(F32),
                                                    ALU.subtract).then_inc(hl_done, 1)
                        yield
                        if c < NC and c % NCH == 0:
                            expert_lo(c // CPE)

                    if setup:
                        link(nc.gpsimd.memset(half[:, :], -0.5))
                        for buf in (axh[:, L:XW], axl[:, L:XW], k3[:, :, L:XW]):
                            link(nc.gpsimd.memset(buf.bitcast(F32), 0.0))
                    interleave("pool", pool, link, [lambda c=c: chunk(c) for c in range(steps_n)])

            nc.all_engine_barrier()
            nums = sorted(s.num for s in sems)
            nc.gpsimd.sem_clear(range(nums[0], nums[-1] + 1))
            nc.all_engine_barrier()

        T_SSM, T_ATT = dict(t_head=24), dict(t_att=0.5)

        def ssm_phase(load):
            return Phase(main=0, fin=(x1, x2), ssm=True, pre=True, slot=1, x_out=x1, load=load, t_pre=16.5,
                         hh_act=HH_SSM, form=FORM_SSM, **T_SSM)

        def att_phase(store):
            return Phase(main=1, fin=(x3, x3), att=True, slot=0, x_out=x3, store=store, hh_act=HH_ATT, form=FORM_ATT,
                         **T_ATT)

        run_block([Phase(ssm=True, slot=0, x_out=x2, load=(0, 0), **T_SSM)], setup=True)
        run_block([Phase(main=0, ssm=True, slot=1, x_out=x1, load=(0, 1), hh_act=HH_SSM, form=FORM_SSM, **T_SSM),
                   Phase(main=1, fin=(x2, x2), pre=True, att=True, slot=0, x_out=x3, t_pre=6, t_att=15, pace=EDGE_PACE,
                         hh_act=HH_ATT, form=FORM_ATT)])
        with nc.Fori(0, B // 2 - 1) as j:
            run_block([ssm_phase((j + 1, 0)), att_phase((j, 0)), ssm_phase((j + 1, 1)), att_phase((j, 1))])
        run_block([Phase(main=0, fin=(x1, x2), pre=True, att=True, slot=1, x_out=x1, t_pre=1, t_att=10, pace=EDGE_PACE,
                         hh_act=HH_ATT, form=FORM_ATT),
                   Phase(main=1, fin=(x3, x3), store=(B // 2 - 1, 0))])
        run_block([Phase(fin=(x1, x1), store=(B // 2 - 1, 1))])


def _pack(w):
    out = np.zeros((P, NPACK), np.float32)

    def put(name, a):
        at, n = _COLS[name]
        a = np.asarray(a)
        out[:a.shape[0], at:at + a.shape[1]] = a

    a_ = "L0_attn_a_"
    b_ = "L0_attn_b_"
    w_x = w[a_ + "W_xproj"]
    put("w_in", w[a_ + "W_in"].T)
    put("w_bc", np.concatenate([w_x[DTRANK:].T] * 2, 0))
    put("w_dtx", np.concatenate([w_x[:DTRANK]] * 2, 1))
    put("w_dt", np.concatenate([w[a_ + "W_dt"].T] * 2, 1))
    put("k_conv", np.concatenate([w[a_ + "Kx"][:, 0, :], w[a_ + "Kz"][:, 0, :]], 0))
    put("b_dt", np.concatenate([w[a_ + "b_dt"]] * 2)[:, None])
    put("a_log", w[a_ + "A_log"].reshape(INNER, KT, 2).transpose(2, 0, 1).reshape(P, KT))
    put("d_skip", w[a_ + "D"][:, None])
    w_out = w[a_ + "W_out"].T
    put("w_out_y", np.concatenate([w_out[:INNER]] * 2, 0))
    put("w_out_z", w_out[INNER:])
    put("w_route", np.concatenate([w["L0_ffn_w_router"], w["L0_ffn_w_gating"]], 1))
    put("w_q", w[b_ + "Wq"].T)
    put("w_k", w[b_ + "Wk"].T)
    for v in "qk":
        put("b_" + v, np.repeat(w[b_ + "b" + v].reshape(4, 4, 1, HD), 4, 2).reshape(4, P).T)
    put("w_v", w[b_ + "Wv"].T)
    put("b_v", np.repeat(w[b_ + "bv"][None, :], P, 0))
    put("w_o", w[b_ + "Wo"].T)
    put("b_o", np.repeat(w[b_ + "bo"][None, :], P, 0))
    put("ident", np.eye(P))
    q, k = np.arange(QT)[:, None], np.arange(KW)[None, :]
    ok = (k >= q) & (k - LEFT < (q // CHUNK + 1) * CHUNK)
    put("mask", np.where(ok, 0.0, NEG))
    put("sel", np.concatenate([np.eye(E)] * 6, 0))
    put("lo_ssm", (np.arange(P) >= INNER)[:, None])
    copy = np.arange(P) // HD % 4
    put("lo_q", (copy >= 2)[:, None])
    put("lo_k", (copy % 2 == 1)[:, None])
    return out


def kernel(**inputs):
    import concourse.bacc as bacc
    from concourse.bass_utils import run_bass_kernel_spmd as run

    w = {k: np.asarray(v) for k, v in inputs.items()}
    arrays = {"x": w["L0_attn_a_x"], "pack": _pack(w), "w_gate": w["L0_ffn_w_gate"],
              "w_up": w["L0_ffn_w_up"], "w_down": w["L0_ffn_w_down"]}
    nc = bacc.Bacc("TRN2", target_bir_lowering=False, num_devices=1)
    aps = [nc.dram_tensor("in_" + n, a.shape, F32, kind="ExternalInput").ap() for n, a in arrays.items()]
    out = nc.dram_tensor("out", (B, L, D), F32, kind="ExternalOutput").ap()
    build(nc, *aps, out)
    r = run(nc, [{"in_" + n: np.ascontiguousarray(a) for n, a in arrays.items()}], core_ids=[0])
    return r.results[0]["out"]
```
